# Optimizing a Trainium2 kernel written in Bass

```python
import numpy as np
import jax
import jax.numpy as jnp

def _softmax(x, axis=-1):
    return jax.nn.softmax(x, axis=axis)

def _gelu(x):
    return jax.nn.gelu(x, approximate=True)

def _silu(x):
    return jax.nn.silu(x)

def _sigmoid(x):
    return jax.nn.sigmoid(x)

def _layernorm(x, axis=-1, eps=1e-05):
    m = jnp.mean(x, axis=axis, keepdims=True)
    v = jnp.var(x, axis=axis, keepdims=True)
    return (x - m) / jnp.sqrt(v + eps)

def _scatter_add(tgt, idx, src, axis=0):
    return tgt.at[idx].add(src)

def _segment_sum(src, seg, n):
    return jax.ops.segment_sum(src, seg, n)
kernel_name = 'mk_dlrm_tower_d1_rec_r8_64a30c'

def setup_inputs(seed: int=0):
    np.random.seed(seed)
    _w = jnp.asarray

    def _rec_inputs():
        import jax
        import jax.numpy as jnp
        _tk = jax.random.key(seed)
        ids = jnp.stack([jax.random.randint(jax.random.fold_in(_tk, 200 + f), (2048,), 0, v, jnp.int32) for f, v in enumerate([1000, 1250, 1000, 125000, 1250, 12500, 1000, 1000, 12500, 12500, 1250, 1250, 1000, 1000, 12500, 1250, 12500, 12500, 1000, 12500, 1000, 12500, 1000, 1000, 1000, 1000])], axis=1)
        tbl_0 = 0.05 * jax.random.normal(jax.random.fold_in(_tk, 500 + 0), (1000, 128), jnp.float32)
        tbl_1 = 0.05 * jax.random.normal(jax.random.fold_in(_tk, 500 + 1), (1250, 128), jnp.float32)
        tbl_2 = 0.05 * jax.random.normal(jax.random.fold_in(_tk, 500 + 2), (1000, 128), jnp.float32)
        tbl_3 = 0.05 * jax.random.normal(jax.random.fold_in(_tk, 500 + 3), (125000, 128), jnp.float32)
        tbl_4 = 0.05 * jax.random.normal(jax.random.fold_in(_tk, 500 + 4), (1250, 128), jnp.float32)
        tbl_5 = 0.05 * jax.random.normal(jax.random.fold_in(_tk, 500 + 5), (12500, 128), jnp.float32)
        tbl_6 = 0.05 * jax.random.normal(jax.random.fold_in(_tk, 500 + 6), (1000, 128), jnp.float32)
        tbl_7 = 0.05 * jax.random.normal(jax.random.fold_in(_tk, 500 + 7), (1000, 128), jnp.float32)
        tbl_8 = 0.05 * jax.random.normal(jax.random.fold_in(_tk, 500 + 8), (12500, 128), jnp.float32)
        tbl_9 = 0.05 * jax.random.normal(jax.random.fold_in(_tk, 500 + 9), (12500, 128), jnp.float32)
        tbl_10 = 0.05 * jax.random.normal(jax.random.fold_in(_tk, 500 + 10), (1250, 128), jnp.float32)
        tbl_11 = 0.05 * jax.random.normal(jax.random.fold_in(_tk, 500 + 11), (1250, 128), jnp.float32)
        tbl_12 = 0.05 * jax.random.normal(jax.random.fold_in(_tk, 500 + 12), (1000, 128), jnp.float32)
        tbl_13 = 0.05 * jax.random.normal(jax.random.fold_in(_tk, 500 + 13), (1000, 128), jnp.float32)
        tbl_14 = 0.05 * jax.random.normal(jax.random.fold_in(_tk, 500 + 14), (12500, 128), jnp.float32)
        tbl_15 = 0.05 * jax.random.normal(jax.random.fold_in(_tk, 500 + 15), (1250, 128), jnp.float32)
        tbl_16 = 0.05 * jax.random.normal(jax.random.fold_in(_tk, 500 + 16), (12500, 128), jnp.float32)
        tbl_17 = 0.05 * jax.random.normal(jax.random.fold_in(_tk, 500 + 17), (12500, 128), jnp.float32)
        tbl_18 = 0.05 * jax.random.normal(jax.random.fold_in(_tk, 500 + 18), (1000, 128), jnp.float32)
        tbl_19 = 0.05 * jax.random.normal(jax.random.fold_in(_tk, 500 + 19), (12500, 128), jnp.float32)
        tbl_20 = 0.05 * jax.random.normal(jax.random.fold_in(_tk, 500 + 20), (1000, 128), jnp.float32)
        tbl_21 = 0.05 * jax.random.normal(jax.random.fold_in(_tk, 500 + 21), (12500, 128), jnp.float32)
        tbl_22 = 0.05 * jax.random.normal(jax.random.fold_in(_tk, 500 + 22), (1000, 128), jnp.float32)
        tbl_23 = 0.05 * jax.random.normal(jax.random.fold_in(_tk, 500 + 23), (1000, 128), jnp.float32)
        tbl_24 = 0.05 * jax.random.normal(jax.random.fold_in(_tk, 500 + 24), (1000, 128), jnp.float32)
        tbl_25 = 0.05 * jax.random.normal(jax.random.fold_in(_tk, 500 + 25), (1000, 128), jnp.float32)
        _rk = jax.random.fold_in(_tk, 7)
        r_dense_features = -0.000520686 + 1.00062 * jax.random.normal(jax.random.fold_in(_rk, 101), (2048, 128), jnp.float32)
        W_top1 = 0.0405887 * jax.random.normal(jax.random.fold_in(_tk, 801), (607, 512), jnp.float32)
        W_top2 = 0.0441942 * jax.random.normal(jax.random.fold_in(_tk, 802), (512, 256), jnp.float32)
        W_top3 = 0.0625 * jax.random.normal(jax.random.fold_in(_tk, 803), (256, 1), jnp.float32)
        b_top1 = jnp.zeros((512,), jnp.float32)
        b_top2 = jnp.zeros((256,), jnp.float32)
        return (r_dense_features, ids, tbl_0, tbl_1, tbl_2, tbl_3, tbl_4, tbl_5, tbl_6, tbl_7, tbl_8, tbl_9, tbl_10, tbl_11, tbl_12, tbl_13, tbl_14, tbl_15, tbl_16, tbl_17, tbl_18, tbl_19, tbl_20, tbl_21, tbl_22, tbl_23, tbl_24, tbl_25, W_top1, b_top1, W_top2, b_top2, W_top3)
    r_dense_features, ids, tbl_0, tbl_1, tbl_2, tbl_3, tbl_4, tbl_5, tbl_6, tbl_7, tbl_8, tbl_9, tbl_10, tbl_11, tbl_12, tbl_13, tbl_14, tbl_15, tbl_16, tbl_17, tbl_18, tbl_19, tbl_20, tbl_21, tbl_22, tbl_23, tbl_24, tbl_25, W_top1, b_top1, W_top2, b_top2, W_top3 = _rec_inputs()

    def _L0_rec_setup():
        import jax, jax.numpy as jnp
        import numpy as np
        B, F, D = (2048, 26, 128)
        key = jax.random.key(seed)
        k1, k2 = jax.random.split(key)
        dense_features = jax.random.normal(k1, (B, D), dtype=jnp.float32)
        sparse_values = jax.random.normal(k2, (B, F, D), dtype=jnp.float32)
        return {'dense_features': dense_features, 'sparse_values': sparse_values}
    _L0_rec_all = _L0_rec_setup()
    _L0_rec_in = {k: v for k, v in _L0_rec_all.items() if k in ()}
    del _L0_rec_all
    return {'r_dense_features': r_dense_features, 'ids': ids, 'tbl_0': tbl_0, 'tbl_1': tbl_1, 'tbl_2': tbl_2, 'tbl_3': tbl_3, 'tbl_4': tbl_4, 'tbl_5': tbl_5, 'tbl_6': tbl_6, 'tbl_7': tbl_7, 'tbl_8': tbl_8, 'tbl_9': tbl_9, 'tbl_10': tbl_10, 'tbl_11': tbl_11, 'tbl_12': tbl_12, 'tbl_13': tbl_13, 'tbl_14': tbl_14, 'tbl_15': tbl_15, 'tbl_16': tbl_16, 'tbl_17': tbl_17, 'tbl_18': tbl_18, 'tbl_19': tbl_19, 'tbl_20': tbl_20, 'tbl_21': tbl_21, 'tbl_22': tbl_22, 'tbl_23': tbl_23, 'tbl_24': tbl_24, 'tbl_25': tbl_25, 'W_top1': W_top1, 'b_top1': b_top1, 'W_top2': W_top2, 'b_top2': b_top2, 'W_top3': W_top3}

def reference(r_dense_features, ids, tbl_0, tbl_1, tbl_2, tbl_3, tbl_4, tbl_5, tbl_6, tbl_7, tbl_8, tbl_9, tbl_10, tbl_11, tbl_12, tbl_13, tbl_14, tbl_15, tbl_16, tbl_17, tbl_18, tbl_19, tbl_20, tbl_21, tbl_22, tbl_23, tbl_24, tbl_25, W_top1, b_top1, W_top2, b_top2, W_top3):
    import jax
    import jax.numpy as jnp

    def _L0_rec_ref(dense_features, sparse_values):
        import jax, jax.numpy as jnp
        import numpy as np
        B, F, D = (2048, 26, 128)
        sd = jnp.einsum('bfd,bd->bf', sparse_values, dense_features)
        ss = jnp.einsum('bfd,bgd->bfg', sparse_values, sparse_values)
        iu, ju = jnp.triu_indices(F, k=1)
        pairs = ss[:, iu, ju]
        return jnp.concatenate([dense_features, sd, pairs], axis=1)
    e = jnp.stack([tbl_0[ids[:, 0]], tbl_1[ids[:, 1]], tbl_2[ids[:, 2]], tbl_3[ids[:, 3]], tbl_4[ids[:, 4]], tbl_5[ids[:, 5]], tbl_6[ids[:, 6]], tbl_7[ids[:, 7]], tbl_8[ids[:, 8]], tbl_9[ids[:, 9]], tbl_10[ids[:, 10]], tbl_11[ids[:, 11]], tbl_12[ids[:, 12]], tbl_13[ids[:, 13]], tbl_14[ids[:, 14]], tbl_15[ids[:, 15]], tbl_16[ids[:, 16]], tbl_17[ids[:, 17]], tbl_18[ids[:, 18]], tbl_19[ids[:, 19]], tbl_20[ids[:, 20]], tbl_21[ids[:, 21]], tbl_22[ids[:, 22]], tbl_23[ids[:, 23]], tbl_24[ids[:, 24]], tbl_25[ids[:, 25]]], axis=1)
    z = _L0_rec_ref(r_dense_features, e)
    z = z.reshape(z.shape[0], -1)
    h = jnp.concatenate([z, r_dense_features], axis=1)
    h = jnp.maximum(h @ W_top1 + b_top1, 0.0)
    h = jnp.maximum(h @ W_top2 + b_top2, 0.0)
    y = h @ W_top3
    return y

_drawn_inputs = setup_inputs


def setup_inputs(seed=0):
    import zlib

    import numpy as np

    out = dict(_drawn_inputs(seed))
    spreads = {'b_top1': (0.0, 0.1), 'b_top2': (0.0, 0.1)}
    factors = {}
    for name, (base, spread) in spreads.items():
        noise = np.random.default_rng([zlib.crc32(name.encode()), seed]).standard_normal(out[name].shape)
        drawn = base * np.exp(spread * noise) if base else spread * noise
        out[name] = jnp.asarray(drawn.astype(out[name].dtype))
    for name, factor in factors.items():
        out[name] = (out[name] * factor).astype(out[name].dtype)
    return out
```

```python
from contextlib import ExitStack

import numpy as np
import concourse.bass as bass
import concourse.mybir as mybir

ALU = mybir.AluOpType
ACT = mybir.ActivationFunctionType
F32 = mybir.dt.float32
F32R = mybir.dt.float32r
F16 = mybir.dt.float16
I32 = mybir.dt.int32

P = 128
TABLES = 26
FIELDS = TABLES + 1
SLOTS = 32
TILES_PER_BLOCK = 4
BLOCK = TILES_PER_BLOCK * P
QUAD = 4
GROUPS = P // QUAD
BATCH = 4
BATCHES = GROUPS // BATCH
COLS = FIELDS - 1
PAIRS = FIELDS * (FIELDS - 1) // 2
CHUNKS = 3
PC = PAIRS // CHUNKS
assert PC * CHUNKS == PAIRS and PC <= P


SELECTED = [12, 13, 22, 23, 24, 25]
NS = len(SELECTED)
SELECTED_ROWS = 1000
CELLS = 8
CP = SELECTED_ROWS // CELLS
RING = 4


def in_runs(fields, longest):
    out = []
    for f in fields:
        if out and out[-1][-1] == f - 1 and len(out[-1]) < longest:
            out[-1].append(f)
        else:
            out.append([f])
    return out


LOTS = in_runs([t + 1 for t in range(TABLES) if t not in SELECTED], 4)
SELECTED_RUNS = in_runs([t + 1 for t in SELECTED], NS)
NL = len(LOTS)

WORK = {
    (0, 0): ("s", 0), (0, 2): ("s", 1), (0, 4): ("s", 2),
    (1, 0): ("r", 0), (1, 2): ("s", 3), (1, 4): ("r", 1),
    (2, 0): ("r", 2), (2, 2): ("s", 4), (2, 4): ("r", 3),
    (3, 0): ("r", 4), (3, 1): ("s", 5), (3, 2): ("r", 5), (3, 4): ("r", 6),
}


def pair_runs():
    runs, at = [], 0
    for f in range(FIELDS - 1):
        g = f + 1
        while g < FIELDS:
            n = min(FIELDS - g, PC - at % PC)
            runs.append((f, g, n, at // PC, at % PC))
            at += n
            g += n
    assert at == PAIRS
    return runs


RUNS = pair_runs()


def dlrm_tower(nc, r_dense_features, ids, tables, W_top1, b_top1, W_top2, b_top2, W_top3, out):
    B = r_dense_features.shape[0]
    N1, N2 = W_top1.shape[1], W_top2.shape[1]
    TILES = B // P
    BLOCKS = TILES // TILES_PER_BLOCK
    C1, C2 = N1 // P, N2 // P
    assert B == BLOCKS * BLOCK and W_top1.shape[0] == 2 * P + PAIRS
    assert all(tables[t].shape[0] == SELECTED_ROWS == CP * CELLS for t in SELECTED)

    ids_v = ids.rearrange("(p t) f -> p t f", p=P)
    x_v = r_dense_features.rearrange("(p t) d -> p (t d)", p=P)
    out_v = out.rearrange("(p t) o -> p (t o)", p=P)
    gram_dram = nc.dram_tensor("gram_dram", [P, COLS * P], F32, kind="Internal").ap()
    gram_by_field = gram_dram.rearrange("(i f) (g s) -> f g i s", i=QUAD, g=COLS)

    with ExitStack() as ctx:
        def sb(name, shape, dt=F32):
            return ctx.enter_context(nc.sbuf_tensor(name, shape, dt))

        def pb(name, shape):
            return ctx.enter_context(nc.psum_tensor(name, shape, F32))

        def sem(name):
            return ctx.enter_context(nc.semaphore(name))

        ids_all = sb("ids_all", [P, TILES, TABLES], I32)
        ids_now = sb("ids_now", [P, TILES_PER_BLOCK, TABLES], I32)
        ids_half = sb("ids_half", [P, NS, TILES], F16)
        row_int = sb("row_int", [P, CELLS], I32)
        row_of = sb("row_of", [P, CELLS])
        xT = sb("xT", [P, BLOCKS, BLOCK])
        rows = sb("rows", [P, 2, TABLES - NS, P])
        raw = sb("raw", [P, 2, CELLS * P])
        table_hi = sb("table_hi", [P, NS, CELLS, P], F32R)
        table_lo = sb("table_lo", [P, NS, CELLS, P], F32R)
        spread = sb("spread", [P, 2, BLOCK], F16)
        onehot = sb("onehot", [P, RING, BLOCK], F32R)
        chosen = sb("chosen", [P, 2, NS, BLOCK])
        eT = sb("eT", [P, 2, GROUPS, QUAD, SLOTS])
        gram = sb("gram", [P, COLS, TILES_PER_BLOCK, GROUPS])
        pairs = sb("pairs", [P, CHUNKS, QUAD, P])
        w1d = sb("w1d", [P, N1])
        w1p = sb("w1p", [P, CHUNKS, N1])
        w2 = sb("w2", [P, C1, N2])
        w3 = sb("w3", [P, C2])
        b1 = sb("b1", [P, C1])
        b2 = sb("b2", [P, C2])
        h1T = sb("h1T", [P, C1, BLOCK])
        h2T = sb("h2T", [P, C2, BLOCK])
        y_all = sb("y_all", [P, TILES])
        ident = sb("ident", [P, P])
        ident_half = sb("ident_half", [P, P], F16)
        x_rows = gram[:, :, :, :].rearrange("p g t q -> p (g t q)")[:, 0:TILES * P]
        w1x = h1T[:, 0:2, :]

        turned = [pb(f"turned{i}", [P, 4, P]) for i in range(2)]
        product = [pb(f"product{i}", [P, 512]) for i in range(2)]
        layer_ps = [pb(f"layer_ps{i}", [P, 512]) for i in range(2)]
        spread_ps = pb("spread_ps", [P, TILES_PER_BLOCK, P])
        chosen_ps = pb("chosen_ps", [P, 512])

        ids_in = sem("ids_in")
        x_in = sem("x_in")
        w_in = sem("w_in")
        raw_in = [sem(f"raw_in{i}") for i in range(2)]
        ident_clear = sem("ident_clear")
        ident_ready = sem("ident_ready")
        row_int_ready = sem("row_int_ready")
        row_of_ready = sem("row_of_ready")
        ident_half_ready = sem("ident_half_ready")
        ids_half_ready = sem("ids_half_ready")
        ids_copied = sem("ids_copied")
        table_hi_ready = sem("table_hi_ready")
        table_lo_ready = sem("table_lo_ready")
        landed = [[sem(f"landed{i}_{n}") for n in range(NL)] for i in range(2)]
        lots_turned = sem("lots_turned")
        pads_clear = sem("pads_clear")
        w1d_ready = sem("w1d_ready")
        xT_filled = [sem("xT_filled_dve"), sem("xT_filled_act")]
        spread_ready = sem("spread_ready")
        spread_out = sem("spread_out")
        onehots_made = sem("onehots_made")
        onehots_used = sem("onehots_used")
        chosen_out = sem("chosen_out")
        eT_filled = [sem("eT_filled_dve"), sem("eT_filled_act")]
        eT_rest = sem("eT_rest")
        products_ready = sem("products_ready")
        products_out = [sem("products_out_dve"), sem("products_out_act")]
        gram_stored = sem("gram_stored")
        gram_free = sem("gram_free")
        pairs_in = sem("pairs_in")
        layer_ready = sem("layer_ready")
        layer_out = [sem("layer_out_dve"), sem("layer_out_act")]
        out_done = sem("out_done")
        pool_passed = sem("pool_passed")
        sp_passed = sem("sp_passed")

        LOTS_PER_BLOCK = NL * TILES_PER_BLOCK
        BATCHES_PER_BLOCK = BATCHES * TILES_PER_BLOCK
        CELLS_PER_BLOCK = NS * CELLS
        LAYERS = C1 + C2 + 1
        DVE_LAYERS, ACT_LAYERS = (LAYERS + 1) // 2, LAYERS // 2
        WEIGHTS = 7
        assert LOTS_PER_BLOCK % 2 == 0
        row_slot = {f: n for n, f in enumerate(f for lot in LOTS for f in lot)}

        def wait(eng, semaphore, b, per_block, more):
            if isinstance(b, int) and per_block * b + more <= 0:
                return
            eng.wait_ge(semaphore, b * per_block + more)

        def lots_of(j, who):
            return [n for n in range(NL) if (NL * j + n) % 2 == who]

        def by_member(samples):
            return samples.rearrange("p (i t q) -> p i t q", i=QUAD, q=GROUPS)

        def all_blocks(eng, steps):
            steps(0, False, True)
            with eng.Fori(1, BLOCKS - 1) as b:
                steps(b, True, True)
            steps(BLOCKS - 1, True, False)

        block = ctx.enter_context(nc.Block())

        @block.sync
        def _(sp):
            sp.dma_start(ids_all[:, :, :], ids_v).then_inc(ids_in, 16)
            sp.dma_start(x_rows, x_v).then_inc(x_in, 16)
            for k, t in enumerate(SELECTED):
                if k >= 2:
                    sp.wait_ge(table_hi_ready, k - 1)
                    sp.wait_ge(table_lo_ready, k - 1)
                sp.dma_start(raw[0:CP, k % 2, :], tables[t].rearrange("(p c) d -> p (c d)", p=CP))\
                  .then_inc(raw_in[k % 2], 16)
            sp.dma_start(w1x[:, 0, :], W_top1[0:P, :]).then_inc(w_in, 16)
            sp.dma_start(w1x[:, 1, :], W_top1[P + PAIRS:2 * P + PAIRS, :]).then_inc(w_in, 16)
            sp.dma_start(w1p[0:PC, :, :], W_top1[P:P + PAIRS, :].rearrange("(c p) n -> p c n", p=PC))\
              .then_inc(w_in, 16)
            sp.dma_start(w2[:, :, :], W_top2.rearrange("(c p) n -> p c n", p=P)).then_inc(w_in, 16)
            sp.dma_start(w3[:, :], W_top3.rearrange("(c p) o -> p (c o)", p=P),
                         allow_slow_non_contiguous=True).then_inc(w_in, 16)
            sp.dma_start(b1[:, :], b_top1.rearrange("(c p) -> p c", p=P),
                         allow_slow_non_contiguous=True).then_inc(w_in, 16)
            sp.dma_start(b2[:, :], b_top2.rearrange("(c p) -> p c", p=P),
                         allow_slow_non_contiguous=True).then_inc(w_in, 16)

            def steps(b, before, after):
                if before:
                    wait(sp, layer_ready, b, LAYERS, C1 + 1 - LAYERS)
                    sp.sem_inc(sp_passed, 1)
                for who in range(2):
                    wait(sp, products_out[who], b, BATCHES_PER_BLOCK, BATCHES_PER_BLOCK)
                sp.sem_inc(sp_passed, 1)
                sp.dma_start(gram_dram, gram[:, :, :, :].rearrange("p g t q -> p (g t q)"))\
                  .then_inc(gram_stored, 16)
                wait(sp, gram_stored, b, 16, 16)
                sp.sem_inc(gram_free, 1)
                for f, g, n, c, row in RUNS:
                    sp.dma_start(pairs[row:row + n, c, :, :], gram_by_field[f, g - 1:g - 1 + n, :, :])\
                      .then_inc(pairs_in, 16)

            all_blocks(sp, steps)
            sp.wait_ge(layer_out[0], BLOCKS * DVE_LAYERS + 1)
            sp.dma_start(out_v, y_all[:, :]).then_inc(out_done, 16)
            sp.wait_ge(out_done, 16)

        @block.gpsimd
        def _(pool):
            nc.gpsimd.memset(ident[:, :], 0.0).then_inc(ident_clear, 1)
            pool.wait_ge(ident_clear, 1)
            nc.gpsimd.affine_select(out=ident[:, :], in_=ident[:, :], compare_op=ALU.not_equal, fill=1.0,
                                    base=0, pattern=[[-1, P]], channel_multiplier=1).then_inc(ident_ready, 1)
            nc.gpsimd.iota(row_int[:, :], pattern=[[1, CELLS]], base=0, channel_multiplier=CELLS)\
              .then_inc(row_int_ready, 1)
            pool.wait_ge(ids_in, 16)

            def steps(b, before, after):
                for j in range(TILES_PER_BLOCK):
                    wait(pool, lots_turned, b, LOTS_PER_BLOCK, BLOCKS + NL * (j - 3))
                    nc.gpsimd.tensor_copy(ids_now[:, j, :], ids_all[:, bass.ds(b * TILES_PER_BLOCK + j, 1), :])\
                      .then_inc(ids_copied, 1)
                    for n, lot in enumerate(LOTS):
                        if n == 0:
                            wait(pool, ids_copied, b, TILES_PER_BLOCK, j + 1)
                        wait(pool, lots_turned, b, LOTS_PER_BLOCK, BLOCKS + NL * (j - 2) + n + 1)
                        pool.sem_inc(pool_passed, 1)
                        for f in lot:
                            nc.gpsimd.indirect_dma_start(
                                out=rows[:, j % 2, row_slot[f], :], out_offset=None, in_=tables[f - 1],
                                in_offset=bass.IndirectOffsetOnAxis(ap=ids_now[:, j, f - 1:f], axis=0),
                            ).then_inc(landed[j % 2][n], 16)

            steps(0, False, True)
            with pool.Fori(1, BLOCKS) as b:
                steps(b, True, True)

        def copy_lot(eng, copy, who, b, j, n):
            if n == lots_of(j, who)[0]:
                wait(eng, products_ready, b, BATCHES_PER_BLOCK, BATCHES * (j - 1))
            f0, k = LOTS[n][0], len(LOTS[n])
            wait(eng, lots_turned, b, LOTS_PER_BLOCK, BLOCKS + NL * j + n + 1)
            copy(eT[:, j % 2, :, :, f0:f0 + k].rearrange("p q i f -> p i q f"),
                 turned[who][:, 0:k, :].rearrange("p f (i q) -> p i q f", i=QUAD)).then_inc(eT_filled[who], 1)

        def copy_products(eng, copy, who, b, j):
            if j == 0 and not (isinstance(b, int) and b == 0):
                wait(eng, gram_free, b, 1, 0)
            for m in range(BATCHES):
                wait(eng, products_ready, b, BATCHES_PER_BLOCK, j * BATCHES + m + 1)
                for i in (2 * who, 2 * who + 1):
                    part = slice(SLOTS * i, SLOTS * (i + 1))
                    src = product[m % 2][part, 0:BATCH * QUAD * COLS]\
                        .rearrange("p (k i g) -> p k i g", k=BATCH, i=QUAD)[:, :, i, :]
                    dst = gram[part, :, j, m * BATCH:(m + 1) * BATCH].rearrange("p g k -> p k g")
                    last = copy(dst, src)
                last.then_inc(products_out[who], 1)

        def result_of(c):
            if c < C1:
                return by_member(h1T[:, c, :]), b1[:, c:c + 1]
            return h2T[:, c - C1, :].rearrange("p (t i q) -> p i t q", i=QUAD, q=GROUPS), b2[:, c - C1:c - C1 + 1]

        @block.vector
        def _(dve):
            nc.vector.memset(eT[:, :, :, :, FIELDS:SLOTS].rearrange("p t q i f -> p (t q i) f"), 0.0)\
              .then_inc(pads_clear, 1)
            dve.wait_ge(row_int_ready, 1)
            nc.vector.tensor_copy(row_of[:, :], row_int[:, :]).then_inc(row_of_ready, 1)
            dve.wait_ge(ident_ready, 1)
            nc.vector.tensor_copy(ident_half[:, :], ident[:, :]).then_inc(ident_half_ready, 1)
            dve.wait_ge(ids_in, 16)
            for k, t in enumerate(SELECTED):
                nc.vector.tensor_copy(ids_half[:, k, :], ids_all[:, :, t]).then_inc(ids_half_ready, 1)
            dve.wait_ge(row_of_ready, 1)
            for k in range(0, BLOCKS, 2):
                dve.wait_ge(lots_turned, k + 1)
                nc.vector.tensor_copy(xT[:, k, :].rearrange("p (i t q) -> p t i q", i=QUAD, q=GROUPS),
                                      turned[0][:, :, :].rearrange("p t (i q) -> p t i q", i=QUAD))\
                  .then_inc(xT_filled[0], 1)
            for who in range(2):
                dve.wait_ge(xT_filled[who], BLOCKS // 2)

            def make_onehots(b, k, cells):
                for c in cells:
                    if c == 0:
                        wait(dve, spread_out, b, NS, k + 1)
                    wait(dve, onehots_used, b, CELLS_PER_BLOCK, k * CELLS + c + 1 - RING)
                    nc.vector.tensor_scalar(onehot[:, c % RING, :], spread[:, k % 2, :], row_of[:, c:c + 1], None,
                                            ALU.is_equal).then_inc(onehots_made, 1)

            def select(b, k):
                make_onehots(b, k, range(RING, CELLS))
                if k + 1 < NS:
                    make_onehots(b, k + 1, range(RING))

            for k in range(NS):
                dve.wait_ge(table_hi_ready, k + 1)
                nc.vector.tensor_tensor(table_lo[0:CP, k, :, :].rearrange("p c d -> p (c d)"), raw[0:CP, k % 2, :],
                                        table_hi[0:CP, k, :, :].rearrange("p c d -> p (c d)").bitcast(F32),
                                        ALU.subtract).then_inc(table_lo_ready, 1)
                if k == 0:
                    make_onehots(0, 0, range(RING))
                select(0, k)
            dve.wait_ge(w_in, 16 * WEIGHTS)
            nc.vector.tensor_tensor(w1d[:, :], w1x[:, 0, :], w1x[:, 1, :], ALU.add).then_inc(w1d_ready, 1)
            dve.wait_ge(w1d_ready, 1)

            def steps(b, before, after):
                if after:
                    make_onehots(b + 1, 0, range(RING))
                for j in range(TILES_PER_BLOCK):
                    for n in range(NL):
                        if n in lots_of(j, 0):
                            copy_lot(dve, nc.vector.tensor_copy, 0, b, j, n)
                        if n == 0:
                            wait(dve, products_ready, b, BATCHES_PER_BLOCK, BATCHES * (j - 1))
                            if j == 0:
                                wait(dve, chosen_out, b, NS, NS)
                            nc.vector.tensor_copy(
                                eT[:, j % 2, :, :, 0].rearrange("p q i -> p i q"),
                                xT[:, bass.ds(b, 1), :].rearrange("p o (i t q) -> p (o t) i q", i=QUAD, q=GROUPS)[:, j, :, :],
                            )
                            k = 0
                            for run in SELECTED_RUNS:
                                for f in run:
                                    last = nc.vector.tensor_copy(
                                        eT[:, j % 2, :, :, f].rearrange("p q i -> p i q"),
                                        chosen[:, bass.ds(b % 2, 1), k, j * P:(j + 1) * P]
                                        .rearrange("p o (i q) -> p (o i) q", i=QUAD))
                                    k += 1
                            last.then_inc(eT_rest, 1)
                        kind, c = WORK.get((j, n), (None, 0))
                        if kind == "s" and after:
                            select(b + 1, c)
                        if kind == "r" and before and c % 2 == 0:
                            result(b - 1, c)
                    copy_products(dve, nc.vector.tensor_copy, 0, b, j)

            def result(b, c):
                wait(dve, layer_ready, b, LAYERS, c + 2)
                if c < C1 + C2:
                    dst, bias = result_of(c)
                    nc.vector.tensor_scalar(dst, by_member(layer_ps[0][:, :]), bias, 0.0, ALU.add, ALU.max)\
                      .then_inc(layer_out[0], 1)
                else:
                    nc.vector.tensor_copy(y_all[:, bass.ds(b * TILES_PER_BLOCK, TILES_PER_BLOCK)],
                                          layer_ps[0][:, 0:TILES_PER_BLOCK]).then_inc(layer_out[0], 1)

            all_blocks(dve, steps)
            for c in range(0, LAYERS, 2):
                result(BLOCKS - 1, c)

        @block.scalar
        def _(act):
            for k in range(1, BLOCKS, 2):
                act.wait_ge(lots_turned, k + 1)
                nc.scalar.copy(xT[:, k, :].rearrange("p (i t q) -> p t i q", i=QUAD, q=GROUPS),
                               turned[1][:, :, :].rearrange("p t (i q) -> p t i q", i=QUAD))\
                  .then_inc(xT_filled[1], 1)

            def copy_spread(b, k):
                wait(act, spread_ready, b, NS, k + 1)
                wait(act, onehots_made, b, CELLS_PER_BLOCK, (k - 1) * CELLS)
                nc.scalar.copy(spread[:, k % 2, :], spread_ps[:, :, :].rearrange("p t s -> p (t s)"))\
                  .then_inc(spread_out, 1)

            def copy_chosen(b, k):
                wait(act, onehots_used, b, CELLS_PER_BLOCK, (k + 1) * CELLS)
                if k == 0:
                    wait(act, eT_rest, b, TILES_PER_BLOCK, -TILES_PER_BLOCK)
                nc.scalar.copy(chosen[:, bass.ds(b % 2, 1), k, :].rearrange("p o s -> p (o s)"),
                               chosen_ps[:, :]).then_inc(chosen_out, 1)

            def select(b, k):
                if k + 1 < NS:
                    copy_spread(b, k + 1)
                copy_chosen(b, k)

            def split(k):
                act.wait_ge(raw_in[k % 2], 16 * (k // 2 + 1))
                nc.scalar.copy(table_hi[0:CP, k, :, :].rearrange("p c d -> p (c d)"), raw[0:CP, k % 2, :])\
                  .then_inc(table_hi_ready, 1)

            copy_spread(0, 0)
            split(0)
            for k in range(NS):
                if k + 1 < NS:
                    split(k + 1)
                select(0, k)
            act.wait_ge(w_in, 16 * WEIGHTS)

            def result(b, c):
                wait(act, layer_ready, b, LAYERS, c + 2)
                dst, bias = result_of(c)
                nc.scalar.activation(dst, by_member(layer_ps[1][:, :]), ACT.Relu, bias=bias)\
                  .then_inc(layer_out[1], 1)

            def steps(b, before, after):
                if after:
                    copy_spread(b + 1, 0)
                for j in range(TILES_PER_BLOCK):
                    for n in range(NL):
                        if n in lots_of(j, 1):
                            copy_lot(act, nc.scalar.copy, 1, b, j, n)
                        kind, c = WORK.get((j, n), (None, 0))
                        if kind == "s" and after:
                            select(b + 1, c)
                        if kind == "r" and before and c % 2 == 1:
                            result(b - 1, c)
                    copy_products(act, nc.scalar.copy, 1, b, j)

            all_blocks(act, steps)
            for c in range(1, LAYERS, 2):
                result(BLOCKS - 1, c)

        @block.tensor
        def _(pe):
            for who in range(2):
                pe.sem_inc(layer_out[who], 1)
            pe.sem_inc(layer_ready, 1)
            pe.wait_ge(ident_ready, 1)
            pe.wait_ge(x_in, 16)
            for k in range(BLOCKS):
                if k >= 2:
                    pe.wait_ge(xT_filled[k % 2], k // 2)
                for t in range(TILES_PER_BLOCK):
                    T = k * TILES_PER_BLOCK + t
                    last = nc.tensor.transpose(turned[k % 2][:, t, :], x_rows[:, T * P:(T + 1) * P], ident[:, :])
                last.then_inc(lots_turned, 1)
            for who in range(2):
                pe.wait_ge(xT_filled[who], BLOCKS // 2)

            def spread_ids(b, k):
                wait(pe, spread_out, b, NS, k)
                for t in range(TILES_PER_BLOCK):
                    column = ids_half[:, k, bass.ds(b * TILES_PER_BLOCK + t, 1)]
                    last = nc.tensor.matmul(spread_ps[:, t, :], column.broadcast_to([P, P]), ident_half[:, :],
                                            start=True, stop=True)
                last.then_inc(spread_ready, 1)

            def select(b, k):
                if k + 1 < NS:
                    spread_ids(b, k + 1)
                wait(pe, chosen_out, b, NS, k)
                for c in range(CELLS):
                    wait(pe, onehots_made, b, CELLS_PER_BLOCK, k * CELLS + c + 1)
                    for part in (table_hi, table_lo):
                        last = nc.tensor.matmul(chosen_ps[:, :], part[0:CP, k, c, :], onehot[0:CP, c % RING, :],
                                                start=(c == 0 and part is table_hi),
                                                stop=(c == CELLS - 1 and part is table_lo))
                    last.then_inc(onehots_used, 1)

            def transpose_lot(b, j, n):
                lot = LOTS[n]
                wait(pe, landed[j % 2][n], b, 32 * len(lot), 16 * len(lot) * (j // 2 + 1))
                who, before = (NL * j + n) % 2, (NL * j + n) // 2
                wait(pe, eT_filled[who], b, LOTS_PER_BLOCK // 2, before)
                for k, f in enumerate(lot):
                    last = nc.tensor.transpose(turned[who][:, k, :], rows[:, j % 2, row_slot[f], :], ident[:, :])
                last.then_inc(lots_turned, 1)

            def multiply(b, j):
                for who in range(2):
                    wait(pe, eT_filled[who], b, LOTS_PER_BLOCK // 2, sum(len(lots_of(t, who)) for t in range(j + 1)))
                wait(pe, eT_rest, b, TILES_PER_BLOCK, j + 1)
                for m in range(BATCHES):
                    for who in range(2):
                        wait(pe, products_out[who], b, BATCHES_PER_BLOCK, j * BATCHES + m - 1)
                    for k in range(BATCH):
                        q = m * BATCH + k
                        last = nc.tensor.matmul(product[m % 2][:, k * QUAD * COLS:(k + 1) * QUAD * COLS],
                                                eT[:, j % 2, q, :, :].rearrange("p i f -> p (i f)"),
                                                eT[:, j % 2, q, :, 1:FIELDS], start=True, stop=True)
                    last.then_inc(products_ready, 1)

            def result(b, c):
                done = {0: DVE_LAYERS, 1: ACT_LAYERS}
                if c < C1:
                    wait(pe, layer_out[c % 2], b, done[c % 2], c // 2 + 1)
                    units = slice(c * P, (c + 1) * P)
                    nc.tensor.matmul(layer_ps[c % 2][:, :], w1d[:, units],
                                     xT[:, bass.ds(b, 1), :].rearrange("p o s -> p (o s)"), start=True, stop=False)
                    if c == 0:
                        wait(pe, pairs_in, b, 16 * len(RUNS), 16 * len(RUNS))
                    for k in range(CHUNKS):
                        last = nc.tensor.matmul(layer_ps[c % 2][:, :], w1p[0:PC, k, units],
                                                pairs[0:PC, k, :, :].rearrange("p i s -> p (i s)"),
                                                start=False, stop=(k == CHUNKS - 1))
                elif c < C1 + C2:
                    for who in range(2):
                        most = C1 // 2 if who != c % 2 else c // 2
                        wait(pe, layer_out[who], b, done[who], most + 1)
                    for k in range(C1):
                        last = nc.tensor.matmul(layer_ps[c % 2][:, :], w2[:, k, (c - C1) * P:(c - C1 + 1) * P],
                                                h1T[:, k, :], start=(k == 0), stop=(k == C1 - 1))
                else:
                    for who in range(2):
                        wait(pe, layer_out[who], b, done[who], (C1 + C2) // 2 + 1)
                    for t in range(TILES_PER_BLOCK):
                        for k in range(C2):
                            last = nc.tensor.matmul(layer_ps[0][:, t:t + 1], h2T[:, k, t * P:(t + 1) * P],
                                                    w3[:, k:k + 1], start=(k == 0), stop=(k == C2 - 1))
                last.then_inc(layer_ready, 1)

            pe.wait_ge(ident_half_ready, 1)
            pe.wait_ge(ids_half_ready, NS)
            spread_ids(0, 0)
            for k in range(NS):
                pe.wait_ge(table_hi_ready, k + 1)
                pe.wait_ge(table_lo_ready, k + 1)
                select(0, k)
            pe.wait_ge(pads_clear, 1)
            pe.wait_ge(w_in, 16 * WEIGHTS)
            pe.wait_ge(w1d_ready, 1)

            def steps(b, before, after):
                if after:
                    spread_ids(b + 1, 0)
                for j in range(TILES_PER_BLOCK):
                    for n in range(NL):
                        transpose_lot(b, j, n)
                        kind, c = WORK.get((j, n), (None, 0))
                        if kind == "s" and after:
                            select(b + 1, c)
                        if kind == "r" and before:
                            result(b - 1, c)
                    multiply(b, j)

            all_blocks(pe, steps)
            for c in range(LAYERS):
                result(BLOCKS - 1, c)

    return nc


def kernel(**inputs):
    import concourse.bacc as bacc
    from concourse.bass_utils import run_bass_kernel_spmd

    names = ["r_dense_features", "ids"] + [f"tbl_{t}" for t in range(TABLES)] + \
            ["W_top1", "b_top1", "W_top2", "b_top2", "W_top3"]
    nc = bacc.Bacc("TRN2", target_bir_lowering=False, num_devices=1)
    arrays, aps = {}, {}
    for name in names:
        a = np.ascontiguousarray(inputs[name])
        arrays[f"in_{name}"] = a
        aps[name] = nc.dram_tensor(f"in_{name}", a.shape, mybir.dt.from_np(a.dtype), kind="ExternalInput").ap()
    out = nc.dram_tensor("out_y", [inputs["ids"].shape[0], 1], F32, kind="ExternalOutput").ap()
    dlrm_tower(nc, aps["r_dense_features"], aps["ids"], [aps[f"tbl_{t}"] for t in range(TABLES)],
               aps["W_top1"], aps["b_top1"], aps["W_top2"], aps["b_top2"], aps["W_top3"], out)
    return run_bass_kernel_spmd(nc, [arrays], core_ids=[0]).results[0]["out_y"]
```

```python
from contextlib import ExitStack

import numpy as np
import concourse.bass as bass
import concourse.mybir as mybir

ALU = mybir.AluOpType
ACT = mybir.ActivationFunctionType
F32 = mybir.dt.float32
F32R = mybir.dt.float32r
F16 = mybir.dt.float16
I32 = mybir.dt.int32

P = 128
TABLES = 26
FIELDS = TABLES + 1
TILES_PER_BLOCK = 4
BLOCK = TILES_PER_BLOCK * P
QUAD = 4
GROUPS = P // QUAD
BATCH = 4
BATCHES = GROUPS // BATCH
COLS = FIELDS - 1
PAIRS = FIELDS * (FIELDS - 1) // 2
CHUNKS = 3
PC = PAIRS // CHUNKS
assert PC * CHUNKS == PAIRS and PC <= P


SELECTED = [7, 12, 13, 22, 23, 24, 25]
NS = len(SELECTED)
SELECTED_ROWS = 1000
CELLS = 8
CP = SELECTED_ROWS // CELLS
LEAD = 3
RING = 7
DOUBLED = 3
assert NS * CELLS % RING == 0


def in_runs(fields, longest):
    out = []
    for f in fields:
        if out and out[-1][-1] == f - 1 and len(out[-1]) < longest:
            out[-1].append(f)
        else:
            out.append([f])
    return out


LOTS = in_runs([t + 1 for t in range(TABLES) if t not in SELECTED], 4)
SELECTED_RUNS = in_runs([t + 1 for t in SELECTED], NS)
NL = len(LOTS)

FIRST, BETWEEN, LAST = (
    {(0, 0): [("t", 1)], (0, 1): [("t", 2)], (0, 2): [("t", 3)], (0, 3): [("t", 4)],
     (0, 4): [("t", 5), ("t", 6), ("d", 0)],
     (1, 1): [("p", 0)], (1, 4): [("s", 0)], (2, 2): [("s", 1)], (3, 0): [("s", 2)], (3, 3): [("s", 3)]},
    {(0, 0): [("u", 4)], (0, 1): [("u", 5)], (0, 2): [("u", 6)], (0, 4): [("d", 0)],
     (1, 0): [("r", 0), ("p", 0)], (1, 1): [("r", 1)], (1, 2): [("s", 0)], (1, 4): [("r", 2)],
     (2, 0): [("r", 3)], (2, 1): [("s", 1)], (2, 2): [("r", 4)], (2, 4): [("s", 2)],
     (3, 0): [("r", 5)], (3, 2): [("r", 6)], (3, 3): [("s", 3)]},
    {(0, 0): [("u", 4)], (0, 1): [("u", 5)], (0, 2): [("u", 6)],
     (1, 0): [("r", 0)], (1, 1): [("r", 1)], (1, 2): [("r", 2)], (1, 3): [("r", 3)],
     (1, 4): [("r", 4)], (2, 0): [("r", 5)], (2, 1): [("r", 6)],
     (3, 1): [("h", 0)], (3, 2): [("h", 1)], (3, 3): [("h", 2), ("h", 3)]},
)


def batches_at(work, j, n):
    if j == 0 or work is LAST and j >= 2:
        return list(range(BATCHES)) if n == 0 else []
    return [m for m in range(BATCHES) if m * NL // BATCHES == n]


def run_width(f):
    return COLS if f == 0 else COLS // 2


def pair_loads():
    loads, at = [], 0
    for f in range(FIELDS - 1):
        width, c, row = run_width(f), at // PC, at % PC
        assert row + width <= PC
        if loads and loads[-1][2:4] == [width, c]:
            loads[-1][1] += 1
        else:
            loads.append([f, 1, width, c, row])
        at += width
    assert at == PAIRS
    return loads


LOADS = pair_loads()


def pair_order():
    order = []
    for f in range(FIELDS - 1):
        for cell in range(f * FIELDS, f * FIELDS + run_width(f)):
            a, b = sorted((cell // COLS, cell % COLS + 1))
            order.append(a * (2 * FIELDS - a - 1) // 2 + b - a - 1)
    assert sorted(order) == list(range(PAIRS))
    return order


def dlrm_tower(nc, r_dense_features, ids, tables, W_top1, b_top1, W_top2, b_top2, W_top3, out):
    B = r_dense_features.shape[0]
    N1, N2 = W_top1.shape[1], W_top2.shape[1]
    TILES = B // P
    BLOCKS = TILES // TILES_PER_BLOCK
    C1, C2 = N1 // P, N2 // P
    assert B == BLOCKS * BLOCK and W_top1.shape[0] == 2 * P + PAIRS
    assert all(tables[t].shape[0] == SELECTED_ROWS == CP * CELLS for t in SELECTED)

    ids_v = ids.rearrange("(p t) f -> p t f", p=P)
    x_v = r_dense_features.rearrange("(p t) d -> p (t d)", p=P)
    out_v = out.rearrange("(p t) o -> p (t o)", p=P)
    gram_dram = nc.dram_tensor("gram_dram", [TILES_PER_BLOCK, FIELDS * COLS, P], F32, kind="Internal").ap()

    with ExitStack() as ctx:
        def sb(name, shape, dt=F32):
            return ctx.enter_context(nc.sbuf_tensor(name, shape, dt))

        def pb(name, shape):
            return ctx.enter_context(nc.psum_tensor(name, shape, F32))

        def sem(name):
            return ctx.enter_context(nc.semaphore(name))

        ids_all = sb("ids_all", [P, TILES, TABLES], I32)
        ids_now = sb("ids_now", [P, TILES_PER_BLOCK, TABLES], I32)
        ids_float = sb("ids_float", [P, NS, TILES])
        diagonal = sb("diagonal", [P, TILES_PER_BLOCK, P], F16)
        ones_half = sb("ones_half", [P, P], F16)
        row_of = sb("row_of", [P, CELLS])
        xT = sb("xT", [P, BLOCKS, BLOCK])
        rows = sb("rows", [P, 2, TABLES - NS, P])
        table_hi = sb("table_hi", [P, NS, CELLS, P], F32R)
        table_lo = sb("table_lo", [P, NS, CELLS, P], F32R)
        spread = sb("spread", [P, 2, BLOCK], F16)
        onehot = sb("onehot", [P, RING, BLOCK], F32R)
        chosen = sb("chosen", [P, DOUBLED + NS, BLOCK])
        eT = sb("eT", [P, 2, GROUPS, QUAD, FIELDS])
        gram = sb("gram", [P, 2, QUAD, COLS, GROUPS])
        pairs = sb("pairs", [P, CHUNKS, BLOCK])
        w1d = sb("w1d", [P, N1])
        w1p = sb("w1p", [P, CHUNKS, N1])
        w2 = sb("w2", [P, C1, N2])
        w3 = sb("w3", [P, C2])
        b1 = sb("b1", [P, C1])
        b2 = sb("b2", [P, C2])
        h1T = sb("h1T", [P, C1, BLOCK])
        h2T = sb("h2T", [P, C2, BLOCK])
        y_all = sb("y_all", [P, TILES])
        ident = sb("ident", [P, P])
        ident_half = sb("ident_half", [P, P], F16)
        row_int = y_all[:, 0:CELLS].bitcast(I32)
        x_rows = chosen[:, :, :].rearrange("p k s -> p (k s)")[:, 0:TILES * P]
        raw = [h2T[:, :, :].rearrange("p c s -> p (c s)"),
               pairs[:, 0:2, :].rearrange("p c s -> p (c s)")]
        w1x = h1T[:, 0:2, :]

        turned = [pb(f"turned{i}", [P, 4, P]) for i in range(2)]
        product = [pb(f"product{i}", [P, 512]) for i in range(2)]
        layer_ps = [pb(f"layer_ps{i}", [P, 512]) for i in range(2)]
        spread_ps = pb("spread_ps", [P, TILES_PER_BLOCK, P])
        chosen_ps = pb("chosen_ps", [P, 512])

        ids_in = sem("ids_in")
        x_in = sem("x_in")
        w_in = sem("w_in")
        raw_in = [sem(f"raw_in{i}") for i in range(2)]
        ident_clear = sem("ident_clear")
        ident_ready = sem("ident_ready")
        row_int_ready = sem("row_int_ready")
        row_of_ready = sem("row_of_ready")
        ident_half_ready = sem("ident_half_ready")
        ids_float_ready = sem("ids_float_ready")
        ones_ready = sem("ones_ready")
        diagonals_made = sem("diagonals_made")
        ids_copied = sem("ids_copied")
        table_hi_ready = sem("table_hi_ready")
        table_lo_ready = sem("table_lo_ready")
        landed = [[sem(f"landed{i}_{n}") for n in range(NL)] for i in range(2)]
        lots_turned = sem("lots_turned")
        w1d_ready = sem("w1d_ready")
        xT_filled = [sem("xT_filled_dve"), sem("xT_filled_act")]
        spread_ready = sem("spread_ready")
        spread_out = sem("spread_out")
        onehots_made = sem("onehots_made")
        onehots_used = sem("onehots_used")
        chosen_out = sem("chosen_out")
        eT_filled = [sem("eT_filled_dve"), sem("eT_filled_act")]
        eT_rest = sem("eT_rest")
        products_ready = sem("products_ready")
        products_out = [sem("products_out_dve"), sem("products_out_act")]
        gram_stored = sem("gram_stored")
        pairs_in = [sem(f"pairs_in{t}") for t in range(TILES_PER_BLOCK)]
        layer_ready = sem("layer_ready")
        layer_out = [sem("layer_out_dve"), sem("layer_out_act")]
        out_done = sem("out_done")
        pool_passed = sem("pool_passed")
        sp_passed = sem("sp_passed")

        LOTS_PER_BLOCK = NL * TILES_PER_BLOCK
        BATCHES_PER_BLOCK = BATCHES * TILES_PER_BLOCK
        CELLS_PER_BLOCK = NS * CELLS
        LAYERS = C1 + C2 + 1
        DVE_LAYERS, ACT_LAYERS = (LAYERS + 1) // 2, LAYERS // 2
        WEIGHTS = 7
        assert LOTS_PER_BLOCK % 2 == 0 and C1 % 2 == 0
        row_slot = {f: n for n, f in enumerate(f for lot in LOTS for f in lot)}

        def wait(eng, semaphore, b, per_block, more):
            if isinstance(b, int) and per_block * b + more <= 0:
                return
            eng.wait_ge(semaphore, b * per_block + more)

        def lots_of(j, who):
            return [n for n in range(NL) if (NL * j + n) % 2 == who]

        T = TILES_PER_BLOCK
        WHOLE, HEAD, MIDDLE, TAIL = (0, T), (0, T - 2), (T - 2, T - 1), (T - 1, T)
        LATE_RUNS = ((BLOCKS, MIDDLE), (BLOCKS + 1, TAIL))

        def samples_of(tiles):
            return (tiles[1] - tiles[0]) * P

        def chosen_slot(b, k):
            return 2 * k + b % 2 if k < DOUBLED else DOUBLED + k

        def all_blocks(eng, steps):
            steps(0, FIRST)
            with eng.Fori(1, BLOCKS - 1) as b:
                steps(b, BETWEEN)
            steps(BLOCKS - 1, LAST)

        block = ctx.enter_context(nc.Block())

        @block.sync
        def _(sp):
            sp.dma_start(ids_all[:, :, :], ids_v).then_inc(ids_in, 16)
            sp.dma_start(x_rows, x_v).then_inc(x_in, 16)
            for k, t in enumerate(SELECTED):
                if k >= 2:
                    sp.wait_ge(table_hi_ready, k - 1)
                    sp.wait_ge(table_lo_ready, k - 1)
                sp.dma_start(raw[k % 2][0:CP, :], tables[t].rearrange("(p c) d -> p (c d)", p=CP))\
                  .then_inc(raw_in[k % 2], 16)
            sp.dma_start(w1x[:, 0, :], W_top1[0:P, :]).then_inc(w_in, 16)
            sp.dma_start(w1x[:, 1, :], W_top1[P + PAIRS:2 * P + PAIRS, :]).then_inc(w_in, 16)
            sp.dma_start(w1p[0:PC, :, :], W_top1[P:P + PAIRS, :].rearrange("(c p) n -> p c n", p=PC))\
              .then_inc(w_in, 16)
            sp.dma_start(w2[:, :, :], W_top2.rearrange("(c p) n -> p c n", p=P)).then_inc(w_in, 16)
            sp.dma_start(w3[:, :], W_top3.rearrange("(c p) o -> p (c o)", p=P),
                         allow_slow_non_contiguous=True).then_inc(w_in, 16)
            sp.dma_start(b1[:, :], b_top1.rearrange("(c p) -> p c", p=P),
                         allow_slow_non_contiguous=True).then_inc(w_in, 16)
            sp.dma_start(b2[:, :], b_top2.rearrange("(c p) -> p c", p=P),
                         allow_slow_non_contiguous=True).then_inc(w_in, 16)

            def steps(b):
                for t in range(TILES_PER_BLOCK):
                    for who in range(2):
                        wait(sp, products_out[who], b, BATCHES_PER_BLOCK // 2, BATCHES // 2 * (t + 1))
                    sp.sem_inc(sp_passed, 1)
                    wait(sp, pairs_in[t], b, 16 * len(LOADS), 0)
                    sp.sem_inc(sp_passed, 1)
                    cells = gram_dram[t].rearrange("(f g) (i q) -> i f g q", g=COLS, i=QUAD)
                    for i in range(QUAD):
                        sp.dma_start(cells[i], gram[FIELDS * i:FIELDS * (i + 1), t % 2, i, :, :])\
                          .then_inc(gram_stored, 16)
                    wait(sp, gram_stored, b, 16 * QUAD * TILES_PER_BLOCK, 16 * QUAD * (t + 1))
                    sp.sem_inc(sp_passed, 1)
                    if t == 1:
                        wait(sp, layer_ready, b, LAYERS, C1 + 1 - LAYERS)
                        sp.sem_inc(sp_passed, 1)
                        bring_back(0)
                    if t >= 1:
                        bring_back(t)

            def bring_back(t):
                cells = gram_dram[t]
                for f0, fields, width, c, row in LOADS:
                    sp.dma_start(pairs[row:row + fields * width, c, t * P:(t + 1) * P],
                                 cells[f0 * FIELDS:f0 * FIELDS + max(width, fields * FIELDS), :]
                                 .rearrange("(f w) s -> f w s", f=fields)[:, 0:width]).then_inc(pairs_in[t], 16)

            steps(0)
            with sp.Fori(1, BLOCKS) as b:
                steps(b)
            sp.wait_ge(layer_out[0], (BLOCKS + 2) * DVE_LAYERS + 1)
            sp.dma_start(out_v, y_all[:, :]).then_inc(out_done, 16)
            sp.wait_ge(out_done, 16)

        @block.gpsimd
        def _(pool):
            nc.gpsimd.memset(ident[:, :], 0.0).then_inc(ident_clear, 1)
            pool.wait_ge(ident_clear, 1)
            nc.gpsimd.affine_select(out=ident[:, :], in_=ident[:, :], compare_op=ALU.not_equal, fill=1.0,
                                    base=0, pattern=[[-1, P]], channel_multiplier=1).then_inc(ident_ready, 1)
            nc.gpsimd.iota(row_int[:, :], pattern=[[1, CELLS]], base=0, channel_multiplier=CELLS)\
              .then_inc(row_int_ready, 1)
            pool.wait_ge(ids_in, 16)

            def steps(b):
                for j in range(TILES_PER_BLOCK):
                    wait(pool, lots_turned, b, LOTS_PER_BLOCK, BLOCKS + NL * (j - 3))
                    nc.gpsimd.tensor_copy(ids_now[:, j, :], ids_all[:, bass.ds(b * TILES_PER_BLOCK + j, 1), :])\
                      .then_inc(ids_copied, 1)
                    for n, lot in enumerate(LOTS):
                        if n == 0:
                            wait(pool, ids_copied, b, TILES_PER_BLOCK, j + 1)
                        wait(pool, lots_turned, b, LOTS_PER_BLOCK, BLOCKS + NL * (j - 2) + n + 1)
                        pool.sem_inc(pool_passed, 1)
                        for f in lot:
                            nc.gpsimd.indirect_dma_start(
                                out=rows[:, j % 2, row_slot[f], :], out_offset=None, in_=tables[f - 1],
                                in_offset=bass.IndirectOffsetOnAxis(ap=ids_now[:, j, f - 1:f], axis=0),
                            ).then_inc(landed[j % 2][n], 16)

            steps(0)
            with pool.Fori(1, BLOCKS) as b:
                steps(b)

        def copy_lot(eng, copy, who, b, j, n):
            if n == lots_of(j, who)[0]:
                wait(eng, products_ready, b, BATCHES_PER_BLOCK, BATCHES * (j - 1))
            f0, k = LOTS[n][0], len(LOTS[n])
            wait(eng, lots_turned, b, LOTS_PER_BLOCK, BLOCKS + NL * j + n + 1)
            copy(eT[:, j % 2, :, :, f0:f0 + k].rearrange("p q i f -> p i q f"),
                 turned[who][:, 0:k, :].rearrange("p f (i q) -> p i q f", i=QUAD)).then_inc(eT_filled[who], 1)

        def copy_products(eng, copy, who, b, j, batches):
            for m in batches:
                if m % 2 != who:
                    continue
                if m == who:
                    wait(eng, gram_stored, b, 16 * QUAD * TILES_PER_BLOCK, 16 * QUAD * (j - 1))
                wait(eng, products_ready, b, BATCHES_PER_BLOCK, j * BATCHES + m + 1)
                copy(gram[0:QUAD * FIELDS, j % 2, :, :, m * BATCH:(m + 1) * BATCH].rearrange("p i g k -> p k (i g)"),
                     product[who][0:QUAD * FIELDS, 0:BATCH * QUAD * COLS].rearrange("p (k c) -> p k c", k=BATCH))\
                    .then_inc(products_out[who], 1)

        def result_of(c, tiles):
            n = samples_of(tiles)
            if c < C1:
                return h1T[:, c, 0:n], b1[:, c:c + 1]
            return h2T[:, c - C1, 0:n], b2[:, c - C1:c - C1 + 1]

        def bank_of(c, who, last_run):
            if last_run and c in (2, 3):
                return turned[who][:, :, :].rearrange("p t s -> p (t s)")
            return layer_ps[who][:, :]

        @block.vector
        def _(dve):
            dve.wait_ge(row_int_ready, 1)
            nc.vector.tensor_copy(row_of[:, :], row_int[:, :]).then_inc(row_of_ready, 1)
            dve.wait_ge(ident_ready, 1)
            nc.vector.tensor_copy(ident_half[:, :], ident[:, :]).then_inc(ident_half_ready, 1)
            dve.wait_ge(ids_in, 16)
            for k, t in enumerate(SELECTED):
                nc.vector.tensor_copy(ids_float[:, k, :], ids_all[:, :, t]).then_inc(ids_float_ready, 1)
            nc.vector.memset(ones_half[:, :], 1.0).then_inc(ones_ready, 1)
            dve.wait_ge(row_of_ready, 1)

            def make_onehots(b, k, cells):
                for c in cells:
                    if c == 0:
                        wait(dve, spread_out, b, NS, k + 1)
                    wait(dve, onehots_used, b, CELLS_PER_BLOCK, k * CELLS + c + 1 - RING)
                    nc.vector.tensor_scalar(onehot[:, (k * CELLS + c) % RING, :], spread[:, k % 2, :], row_of[:, c:c + 1], None,
                                            ALU.is_equal).then_inc(onehots_made, 1)

            def select(b, k):
                make_onehots(b, k, range(LEAD, CELLS))
                if k + 1 < NS:
                    make_onehots(b, k + 1, range(LEAD))

            def lower_part(k):
                dve.wait_ge(table_hi_ready, k + 1)
                nc.vector.tensor_tensor(table_lo[0:CP, k, :, :].rearrange("p c d -> p (c d)"), raw[k % 2][0:CP, :],
                                        table_hi[0:CP, k, :, :].rearrange("p c d -> p (c d)").bitcast(F32),
                                        ALU.subtract).then_inc(table_lo_ready, 1)

            def take_in(k):
                make_onehots(0, k, range(LEAD, CELLS))
                if k + 1 < NS:
                    lower_part(k + 1)
                    make_onehots(0, k + 1, range(LEAD))

            def copy_dense(k):
                dve.wait_ge(lots_turned, k + 1)
                nc.vector.tensor_copy(xT[:, k, :], turned[0][:, :, :].rearrange("p t s -> p (t s)"))\
                  .then_inc(xT_filled[0], 1)

            make_onehots(0, 0, range(LEAD))
            copy_dense(0)
            lower_part(0)
            take_in(0)
            copy_dense(2)
            for who in range(2):
                dve.wait_ge(xT_filled[who], BLOCKS // 2)

            def fill_rest(b, j):
                wait(dve, products_ready, b, BATCHES_PER_BLOCK, BATCHES * (j - 1))
                if j == 0:
                    wait(dve, chosen_out, b, NS, NS)
                nc.vector.tensor_copy(
                    eT[:, j % 2, :, :, 0].rearrange("p q i -> p i q"),
                    xT[:, bass.ds(b, 1), j * P:(j + 1) * P].rearrange("p o (i q) -> p (o i) q", i=QUAD))
                for k, f in enumerate(f for run in SELECTED_RUNS for f in run):
                    last = nc.vector.tensor_copy(
                        eT[:, j % 2, :, :, f].rearrange("p q i -> p i q"),
                        chosen[:, bass.ds(chosen_slot(b, k), 1), j * P:(j + 1) * P]
                        .rearrange("p o (i q) -> p (o i) q", i=QUAD))
                last.then_inc(eT_rest, 1)

            def steps(b, work):
                for j in range(TILES_PER_BLOCK):
                    for n in range(NL):
                        if n in lots_of(j, 0):
                            copy_lot(dve, nc.vector.tensor_copy, 0, b, j, n)
                        if n == 1 and j > 0:
                            fill_rest(b, j)
                        for kind, c in work.get((j, n), []):
                            if kind == "t":
                                take_in(c)
                            if kind == "u":
                                select(b, c)
                            if kind == "s":
                                select(b + 1, c)
                            if kind == "r" and c % 2 == 0:
                                result(b - 1, c, b - 1, WHOLE)
                            if kind == "h" and c % 2 == 0:
                                result(b, c, b, HEAD)
                        if work is not FIRST or j > 0:
                            copy_products(dve, nc.vector.tensor_copy, 0, b, j - 1, batches_at(work, j, n))
                        if ("p", 0) in work.get((j, n), []):
                            make_onehots(b + 1, 0, range(LEAD))
                    if j == 0:
                        fill_rest(b, j)
                    if work is FIRST and j == 0:
                        dve.wait_ge(w_in, 16 * WEIGHTS)
                        nc.vector.tensor_tensor(w1d[:, :], w1x[:, 0, :], w1x[:, 1, :], ALU.add)\
                          .then_inc(w1d_ready, 1)

            def result(p, c, b, tiles):
                n = samples_of(tiles)
                wait(dve, layer_ready, p, LAYERS, c + 2)
                bank = bank_of(c, 0, tiles is TAIL)
                if c < C1 + C2:
                    dst, bias = result_of(c, tiles)
                    nc.vector.tensor_scalar(dst, bank[:, 0:n], bias, 0.0, ALU.add, ALU.max)\
                      .then_inc(layer_out[0], 1)
                else:
                    nc.vector.tensor_copy(y_all[:, bass.ds(b * TILES_PER_BLOCK + tiles[0], n // P)],
                                          bank[:, 0:n // P]).then_inc(layer_out[0], 1)

            all_blocks(dve, steps)
            copy_products(dve, nc.vector.tensor_copy, 0, BLOCKS - 1, TILES_PER_BLOCK - 1, range(BATCHES))
            for c in range(C1, LAYERS, 2):
                result(BLOCKS - 1, c, BLOCKS - 1, HEAD)
            for p, tiles in LATE_RUNS:
                for c in range(0, LAYERS, 2):
                    result(p, c, BLOCKS - 1, tiles)

        @block.scalar
        def _(act):
            def make_diagonal(b, k):
                wait(act, spread_ready, b, NS, k)
                for t in range(TILES_PER_BLOCK):
                    last = nc.scalar.activation(diagonal[:, t, :], ident_half[:, :], ACT.Copy,
                                                scale=ids_float[:, k, bass.ds(b * TILES_PER_BLOCK + t, 1)])
                last.then_inc(diagonals_made, 1)

            def copy_spread(b, k):
                wait(act, spread_ready, b, NS, k + 1)
                wait(act, onehots_made, b, CELLS_PER_BLOCK, (k - 1) * CELLS)
                nc.scalar.copy(spread[:, k % 2, :], spread_ps[:, :, :].rearrange("p t s -> p (t s)"))\
                  .then_inc(spread_out, 1)

            def copy_chosen(b, k):
                wait(act, onehots_used, b, CELLS_PER_BLOCK, (k + 1) * CELLS)
                if k in (0, DOUBLED):
                    wait(act, eT_rest, b, TILES_PER_BLOCK, -TILES_PER_BLOCK if k < DOUBLED else 0)
                nc.scalar.copy(chosen[:, bass.ds(chosen_slot(b, k), 1), :].rearrange("p o s -> p (o s)"),
                               chosen_ps[:, :]).then_inc(chosen_out, 1)

            def select(b, k):
                if k + 1 < NS:
                    copy_spread(b, k + 1)
                if k + 2 < NS:
                    make_diagonal(b, k + 2)
                copy_chosen(b, k)

            def split(k):
                act.wait_ge(raw_in[k % 2], 16 * (k // 2 + 1))
                nc.scalar.copy(table_hi[0:CP, k, :, :].rearrange("p c d -> p (c d)"), raw[k % 2][0:CP, :])\
                  .then_inc(table_hi_ready, 1)

            def take_in(k):
                if k + 1 < NS:
                    split(k + 1)
                select(0, k)

            def copy_dense(k):
                act.wait_ge(lots_turned, k + 1)
                nc.scalar.copy(xT[:, k, :], turned[1][:, :, :].rearrange("p t s -> p (t s)"))\
                  .then_inc(xT_filled[1], 1)

            act.wait_ge(ident_half_ready, 1)
            act.wait_ge(ids_float_ready, NS)
            make_diagonal(0, 0)
            copy_spread(0, 0)
            make_diagonal(0, 1)
            split(0)
            copy_dense(1)
            take_in(0)
            copy_dense(3)

            def result(p, c, b, tiles):
                wait(act, layer_ready, p, LAYERS, c + 2)
                dst, bias = result_of(c, tiles)
                bank = bank_of(c, 1, tiles is TAIL)
                nc.scalar.activation(dst, bank[:, 0:samples_of(tiles)], ACT.Relu, bias=bias)\
                  .then_inc(layer_out[1], 1)

            def steps(b, work):
                for j in range(TILES_PER_BLOCK):
                    for n in range(NL):
                        if n in lots_of(j, 1):
                            copy_lot(act, nc.scalar.copy, 1, b, j, n)
                        for kind, c in work.get((j, n), []):
                            if kind == "t":
                                take_in(c)
                            if kind == "p":
                                copy_spread(b + 1, 0)
                                make_diagonal(b + 1, 1)
                            if kind == "u":
                                select(b, c)
                            if kind == "s":
                                select(b + 1, c)
                            if kind == "r" and c % 2 == 1:
                                result(b - 1, c, b - 1, WHOLE)
                            if kind == "h" and c % 2 == 1:
                                result(b, c, b, HEAD)
                        if work is not FIRST or j > 0:
                            copy_products(act, nc.scalar.copy, 1, b, j - 1, batches_at(work, j, n))
                        if ("d", 0) in work.get((j, n), []):
                            make_diagonal(b + 1, 0)
                if work is FIRST:
                    act.wait_ge(w_in, 16 * WEIGHTS)

            all_blocks(act, steps)
            copy_products(act, nc.scalar.copy, 1, BLOCKS - 1, TILES_PER_BLOCK - 1, range(BATCHES))
            for c in range(C1 + 1, LAYERS, 2):
                result(BLOCKS - 1, c, BLOCKS - 1, HEAD)
            for p, tiles in LATE_RUNS:
                for c in range(1, LAYERS, 2):
                    result(p, c, BLOCKS - 1, tiles)

        @block.tensor
        def _(pe):
            for who in range(2):
                pe.sem_inc(layer_out[who], 1)
            pe.sem_inc(layer_ready, 1)
            def transpose_dense(k):
                if k >= 2:
                    pe.wait_ge(xT_filled[k % 2], k // 2)
                for t in range(TILES_PER_BLOCK):
                    T = k * TILES_PER_BLOCK + t
                    last = nc.tensor.transpose(turned[k % 2][:, t, :], x_rows[:, T * P:(T + 1) * P], ident[:, :])
                last.then_inc(lots_turned, 1)

            def spread_ids(b, k):
                wait(pe, spread_out, b, NS, k)
                wait(pe, diagonals_made, b, NS, k + 1)
                nc.tensor.matmul(spread_ps[:, :, :].rearrange("p t s -> p (t s)"), ones_half[:, :],
                                 diagonal[:, :, :].rearrange("p t s -> p (t s)"),
                                 start=True, stop=True).then_inc(spread_ready, 1)

            def select(b, k):
                if k + 1 < NS:
                    spread_ids(b, k + 1)
                wait(pe, chosen_out, b, NS, k)
                for c in range(CELLS):
                    wait(pe, onehots_made, b, CELLS_PER_BLOCK, k * CELLS + c + 1)
                    for part in (table_hi, table_lo):
                        last = nc.tensor.matmul(chosen_ps[:, :], part[0:CP, k, c, :], onehot[0:CP, (k * CELLS + c) % RING, :],
                                                start=(c == 0 and part is table_hi),
                                                stop=(c == CELLS - 1 and part is table_lo))
                    last.then_inc(onehots_used, 1)

            def transpose_lot(b, j, n):
                lot = LOTS[n]
                wait(pe, landed[j % 2][n], b, 32 * len(lot), 16 * len(lot) * (j // 2 + 1))
                who, before = (NL * j + n) % 2, (NL * j + n) // 2
                wait(pe, eT_filled[who], b, LOTS_PER_BLOCK // 2, before)
                for k, f in enumerate(lot):
                    last = nc.tensor.transpose(turned[who][:, k, :], rows[:, j % 2, row_slot[f], :], ident[:, :])
                last.then_inc(lots_turned, 1)

            def multiply(b, j, batches):
                if 0 in batches:
                    for who in range(2):
                        wait(pe, eT_filled[who], b, LOTS_PER_BLOCK // 2,
                             sum(len(lots_of(t, who)) for t in range(j + 1)))
                    wait(pe, eT_rest, b, TILES_PER_BLOCK, j + 1)
                for m in batches:
                    wait(pe, products_out[m % 2], b, BATCHES_PER_BLOCK // 2, j * BATCHES // 2 + m // 2)
                    for k in range(BATCH):
                        q = m * BATCH + k
                        last = nc.tensor.matmul(product[m % 2][0:QUAD * FIELDS, k * QUAD * COLS:(k + 1) * QUAD * COLS],
                                                eT[:, j % 2, q, :, :].rearrange("p i f -> p (i f)"),
                                                eT[:, j % 2, q, :, 1:FIELDS], start=True, stop=True)
                    last.then_inc(products_ready, 1)

            def pairs_back(b, tiles):
                for t in range(*tiles):
                    wait(pe, pairs_in[t], b, 16 * len(LOADS), 16 * len(LOADS))

            def dense_of(b, tiles):
                return xT[:, bass.ds(b, 1), tiles[0] * P:tiles[1] * P].rearrange("p o s -> p (o s)")

            def pairs_of(k, tiles):
                return pairs[0:PC, k, tiles[0] * P:tiles[1] * P]

            def first_layer_at_once(p, b, tiles):
                n = samples_of(tiles)
                for c in range(C1):
                    if c < 2:
                        wait(pe, layer_out[c], p, (DVE_LAYERS, ACT_LAYERS)[c], 1)
                    nc.tensor.matmul(bank_of(c, c % 2, True)[:, 0:n], w1d[:, c * P:(c + 1) * P],
                                     dense_of(b, tiles), start=True, stop=False)
                pairs_back(b, tiles)
                for c in range(C1):
                    for k in range(CHUNKS):
                        last = nc.tensor.matmul(bank_of(c, c % 2, True)[:, 0:n],
                                                w1p[0:PC, k, c * P:(c + 1) * P],
                                                pairs_of(k, tiles), start=False, stop=(k == CHUNKS - 1))
                    last.then_inc(layer_ready, 1)

            def result(p, c, b, tiles):
                n = samples_of(tiles)
                done = {0: DVE_LAYERS, 1: ACT_LAYERS}
                if c < C1:
                    wait(pe, layer_out[c % 2], p, done[c % 2], c // 2 + 1)
                    units = slice(c * P, (c + 1) * P)
                    nc.tensor.matmul(layer_ps[c % 2][:, 0:n], w1d[:, units], dense_of(b, tiles),
                                     start=True, stop=False)
                    if c == 0:
                        pairs_back(b, tiles)
                    for k in range(CHUNKS):
                        last = nc.tensor.matmul(layer_ps[c % 2][:, 0:n], w1p[0:PC, k, units],
                                                pairs_of(k, tiles), start=False, stop=(k == CHUNKS - 1))
                elif c < C1 + C2:
                    for who in range(2):
                        most = C1 // 2 if who != c % 2 else c // 2
                        wait(pe, layer_out[who], p, done[who], most + 1)
                    for k in range(C1):
                        last = nc.tensor.matmul(layer_ps[c % 2][:, 0:n], w2[:, k, (c - C1) * P:(c - C1 + 1) * P],
                                                h1T[:, k, 0:n], start=(k == 0), stop=(k == C1 - 1))
                else:
                    for who in range(2):
                        wait(pe, layer_out[who], p, done[who], (C1 + C2) // 2 + 1)
                    for t in range(n // P):
                        for k in range(C2):
                            last = nc.tensor.matmul(layer_ps[0][:, t:t + 1], h2T[:, k, t * P:(t + 1) * P],
                                                    w3[:, k:k + 1], start=(k == 0), stop=(k == C2 - 1))
                last.then_inc(layer_ready, 1)

            def take_in(k):
                pe.wait_ge(table_hi_ready, k + 1)
                pe.wait_ge(table_lo_ready, k + 1)
                select(0, k)

            pe.wait_ge(ones_ready, 1)
            spread_ids(0, 0)
            pe.wait_ge(ident_ready, 1)
            pe.wait_ge(x_in, 16)
            transpose_dense(0)
            transpose_dense(1)
            take_in(0)
            transpose_dense(2)
            transpose_dense(3)
            for who in range(2):
                pe.wait_ge(xT_filled[who], BLOCKS // 2)

            def steps(b, work):
                for j in range(TILES_PER_BLOCK):
                    for n in range(NL):
                        transpose_lot(b, j, n)
                        for kind, c in work.get((j, n), []):
                            if kind == "t":
                                take_in(c)
                            if kind == "p":
                                spread_ids(b + 1, 0)
                            if kind == "u":
                                select(b, c)
                            if kind == "s":
                                select(b + 1, c)
                            if kind == "r":
                                result(b - 1, c, b - 1, WHOLE)
                            if kind == "h":
                                result(b, c, b, HEAD)
                        if work is not FIRST or j > 0:
                            multiply(b, j - 1, batches_at(work, j, n))
                if work is FIRST:
                    pe.wait_ge(w_in, 16 * WEIGHTS)
                    pe.wait_ge(w1d_ready, 1)

            all_blocks(pe, steps)
            multiply(BLOCKS - 1, TILES_PER_BLOCK - 1, range(BATCHES))
            for c in range(C1, LAYERS):
                result(BLOCKS - 1, c, BLOCKS - 1, HEAD)
            for c in range(LAYERS):
                result(BLOCKS, c, BLOCKS - 1, MIDDLE)
            first_layer_at_once(BLOCKS + 1, BLOCKS - 1, TAIL)
            for c in range(C1, LAYERS):
                result(BLOCKS + 1, c, BLOCKS - 1, TAIL)

    return nc


def kernel(**inputs):
    import concourse.bacc as bacc
    from concourse.bass_utils import run_bass_kernel_spmd

    names = ["r_dense_features", "ids"] + [f"tbl_{t}" for t in range(TABLES)] + \
            ["W_top1", "b_top1", "W_top2", "b_top2", "W_top3"]
    nc = bacc.Bacc("TRN2", target_bir_lowering=False, num_devices=1)
    arrays, aps = {}, {}
    for name in names:
        a = np.ascontiguousarray(inputs[name])
        if name == "W_top1":
            a = a[np.concatenate([np.arange(P), P + np.array(pair_order()), np.arange(P + PAIRS, a.shape[0])])]
        arrays[f"in_{name}"] = a
        aps[name] = nc.dram_tensor(f"in_{name}", a.shape, mybir.dt.from_np(a.dtype), kind="ExternalInput").ap()
    out = nc.dram_tensor("out_y", [inputs["ids"].shape[0], 1], F32, kind="ExternalOutput").ap()
    dlrm_tower(nc, aps["r_dense_features"], aps["ids"], [aps[f"tbl_{t}"] for t in range(TABLES)],
               aps["W_top1"], aps["b_top1"], aps["W_top2"], aps["b_top2"], aps["W_top3"], out)
    return run_bass_kernel_spmd(nc, [arrays], core_ids=[0]).results[0]["out_y"]
```

```python
from contextlib import ExitStack

import numpy as np
import concourse.bass as bass
import concourse.mybir as mybir

ALU = mybir.AluOpType
ACT = mybir.ActivationFunctionType
F32 = mybir.dt.float32
F32R = mybir.dt.float32r
F16 = mybir.dt.float16
I32 = mybir.dt.int32

P = 128
TABLES = 26
FIELDS = TABLES + 1
TILES_PER_BLOCK = 4
BLOCK = TILES_PER_BLOCK * P
QUAD = 4
GROUPS = P // QUAD
BATCH = 4
BATCHES = GROUPS // BATCH
COLS = FIELDS - 1
PAIRS = FIELDS * (FIELDS - 1) // 2
CHUNKS = 3
PC = PAIRS // CHUNKS
assert PC * CHUNKS == PAIRS and PC <= P


SELECTED = [7, 12, 13, 22, 23, 24, 25]
NS = len(SELECTED)
SELECTED_ROWS = 1000
CELLS = 8
CP = SELECTED_ROWS // CELLS
LEAD = 3
RING = 7
DOUBLED = 3
assert NS * CELLS % RING == 0


def in_runs(fields, longest):
    out = []
    for f in fields:
        if out and out[-1][-1] == f - 1 and len(out[-1]) < longest:
            out[-1].append(f)
        else:
            out.append([f])
    return out


LOTS = in_runs([t + 1 for t in range(TABLES) if t not in SELECTED], 4)
SELECTED_RUNS = in_runs([t + 1 for t in SELECTED], NS)
NL = len(LOTS)

FIRST, BETWEEN, LAST = (
    {(0, 0): [("t", 1)], (0, 1): [("t", 2)], (0, 2): [("t", 3)], (0, 3): [("t", 4)],
     (0, 4): [("t", 5), ("t", 6), ("d", 0)],
     (1, 1): [("p", 0)], (1, 4): [("s", 0)], (2, 2): [("s", 1)], (3, 0): [("s", 2)], (3, 3): [("s", 3)]},
    {(0, 0): [("u", 4)], (0, 1): [("u", 5)], (0, 2): [("u", 6)], (0, 4): [("d", 0)],
     (1, 0): [("r", 0), ("p", 0)], (1, 1): [("r", 1)], (1, 2): [("s", 0)], (1, 4): [("r", 2)],
     (2, 0): [("r", 3)], (2, 1): [("s", 1)], (2, 2): [("r", 4)], (2, 4): [("s", 2)],
     (3, 0): [("r", 5)], (3, 2): [("r", 6)], (3, 3): [("s", 3)]},
    {(0, 0): [("u", 4)], (0, 1): [("u", 5)], (0, 2): [("u", 6)],
     (1, 0): [("r", 0)], (1, 1): [("r", 1)], (1, 2): [("r", 2)], (1, 3): [("r", 3)],
     (1, 4): [("r", 4)], (2, 1): [("r", 5)],
     (3, 0): [("r", 6)], (3, 1): [("h", 0)], (3, 2): [("h", 1)], (3, 3): [("h", 2)], (3, 4): [("h", 3)]},
)


def batches_at(work, j, n):
    if j == 0 or work is LAST and j >= 2:
        return list(range(BATCHES)) if n == 0 else []
    return [m for m in range(BATCHES) if m * NL // BATCHES == n]


def run_width(f):
    return COLS if f == 0 else COLS // 2


def pair_loads():
    loads, at = [], 0
    for f in range(FIELDS - 1):
        width, c, row = run_width(f), at // PC, at % PC
        assert row + width <= PC
        if loads and loads[-1][2:4] == [width, c]:
            loads[-1][1] += 1
        else:
            loads.append([f, 1, width, c, row])
        at += width
    assert at == PAIRS
    return loads


LOADS = pair_loads()
LOADS_OF = [sum(load[3] == c for load in LOADS) for c in range(CHUNKS)]


def pair_order():
    order = []
    for f in range(FIELDS - 1):
        for cell in range(f * FIELDS, f * FIELDS + run_width(f)):
            a, b = sorted((cell // COLS, cell % COLS + 1))
            order.append(a * (2 * FIELDS - a - 1) // 2 + b - a - 1)
    assert sorted(order) == list(range(PAIRS))
    return order


def dlrm_tower(nc, r_dense_features, ids, tables, W_top1, b_top1, W_top2, b_top2, W_top3, out):
    B = r_dense_features.shape[0]
    N1, N2 = W_top1.shape[1], W_top2.shape[1]
    TILES = B // P
    BLOCKS = TILES // TILES_PER_BLOCK
    C1, C2 = N1 // P, N2 // P
    assert B == BLOCKS * BLOCK and W_top1.shape[0] == 2 * P + PAIRS
    assert all(tables[t].shape[0] == SELECTED_ROWS == CP * CELLS for t in SELECTED)

    ids_v = ids.rearrange("(p t) f -> p t f", p=P)
    x_v = r_dense_features.rearrange("(p t) d -> p (t d)", p=P)
    out_v = out.rearrange("(p t) o -> p (t o)", p=P)
    gram_dram = nc.dram_tensor("gram_dram", [TILES_PER_BLOCK, FIELDS * COLS, P], F32, kind="Internal").ap()

    with ExitStack() as ctx:
        def sb(name, shape, dt=F32):
            return ctx.enter_context(nc.sbuf_tensor(name, shape, dt))

        def pb(name, shape):
            return ctx.enter_context(nc.psum_tensor(name, shape, F32))

        def sem(name):
            return ctx.enter_context(nc.semaphore(name))

        ids_all = sb("ids_all", [P, TILES, TABLES], I32)
        ids_now = sb("ids_now", [P, TILES_PER_BLOCK, TABLES], I32)
        ids_float = sb("ids_float", [P, NS, TILES])
        diagonal = sb("diagonal", [P, TILES_PER_BLOCK, P], F16)
        ones_half = sb("ones_half", [P, P], F16)
        row_of = sb("row_of", [P, CELLS])
        xT = sb("xT", [P, BLOCKS, BLOCK])
        rows = sb("rows", [P, 2, TABLES - NS, P])
        table_hi = sb("table_hi", [P, NS, CELLS, P], F32R)
        table_lo = sb("table_lo", [P, NS, CELLS, P], F32R)
        spread = sb("spread", [P, 2, BLOCK], F16)
        onehot = sb("onehot", [P, RING, BLOCK], F32R)
        chosen = sb("chosen", [P, DOUBLED + NS, BLOCK])
        eT = sb("eT", [P, 2, GROUPS, QUAD, FIELDS])
        gram = sb("gram", [P, 2, QUAD, COLS, GROUPS])
        pairs = sb("pairs", [P, CHUNKS, BLOCK])
        w1d = sb("w1d", [P, N1])
        w1p = sb("w1p", [P, CHUNKS, N1])
        w2 = sb("w2", [P, C1, N2])
        w3 = sb("w3", [P, C2])
        b1 = sb("b1", [P, C1])
        b2 = sb("b2", [P, C2])
        h1T = sb("h1T", [P, C1, BLOCK])
        h2T = sb("h2T", [P, C2, BLOCK])
        y_all = sb("y_all", [P, TILES])
        ident = sb("ident", [P, P])
        ident_half = sb("ident_half", [P, P], F16)
        row_int = y_all[:, 0:CELLS].bitcast(I32)
        x_rows = chosen[:, :, :].rearrange("p k s -> p (k s)")[:, 0:TILES * P]
        raw = [h2T[:, :, :].rearrange("p c s -> p (c s)"),
               pairs[:, 0:2, :].rearrange("p c s -> p (c s)")]
        w1x = h1T[:, 0:2, :]

        turned = [pb(f"turned{i}", [P, 4, P]) for i in range(2)]
        product = [pb(f"product{i}", [P, 512]) for i in range(2)]
        layer_ps = [pb(f"layer_ps{i}", [P, 512]) for i in range(2)]
        spread_ps = pb("spread_ps", [P, TILES_PER_BLOCK, P])
        chosen_ps = pb("chosen_ps", [P, 512])

        ids_in = sem("ids_in")
        x_in = sem("x_in")
        w_in = sem("w_in")
        raw_in = [sem(f"raw_in{i}") for i in range(2)]
        ident_clear = sem("ident_clear")
        ident_ready = sem("ident_ready")
        row_int_ready = sem("row_int_ready")
        row_of_ready = sem("row_of_ready")
        ident_half_ready = sem("ident_half_ready")
        ids_float_ready = sem("ids_float_ready")
        ones_ready = sem("ones_ready")
        diagonals_made = sem("diagonals_made")
        ids_copied = sem("ids_copied")
        table_hi_ready = sem("table_hi_ready")
        table_lo_ready = sem("table_lo_ready")
        landed = [[sem(f"landed{i}_{n}") for n in range(NL)] for i in range(2)]
        lots_turned = sem("lots_turned")
        w1d_ready = sem("w1d_ready")
        xT_filled = [sem("xT_filled_dve"), sem("xT_filled_act")]
        spread_ready = sem("spread_ready")
        spread_out = sem("spread_out")
        onehots_made = sem("onehots_made")
        onehots_used = sem("onehots_used")
        chosen_out = sem("chosen_out")
        eT_filled = [sem("eT_filled_dve"), sem("eT_filled_act")]
        eT_rest = sem("eT_rest")
        products_ready = sem("products_ready")
        products_out = [sem("products_out_dve"), sem("products_out_act")]
        gram_stored = sem("gram_stored")
        pairs_in = [[sem(f"pairs_in{t}_{c}") for c in range(CHUNKS)] for t in range(TILES_PER_BLOCK)]
        layer_ready = sem("layer_ready")
        layer_out = [sem("layer_out_dve"), sem("layer_out_act")]
        out_done = sem("out_done")
        pool_passed = sem("pool_passed")
        sp_passed = sem("sp_passed")

        LOTS_PER_BLOCK = NL * TILES_PER_BLOCK
        BATCHES_PER_BLOCK = BATCHES * TILES_PER_BLOCK
        CELLS_PER_BLOCK = NS * CELLS
        LAYERS = C1 + C2 + 1
        DVE_LAYERS, ACT_LAYERS = (LAYERS + 1) // 2, LAYERS // 2
        WEIGHTS = 7
        assert LOTS_PER_BLOCK % 2 == 0 and C1 % 2 == 0
        row_slot = {f: n for n, f in enumerate(f for lot in LOTS for f in lot)}

        def wait(eng, semaphore, b, per_block, more):
            if isinstance(b, int) and per_block * b + more <= 0:
                return
            eng.wait_ge(semaphore, b * per_block + more)

        def lots_of(j, who):
            return [n for n in range(NL) if (NL * j + n) % 2 == who]

        T = TILES_PER_BLOCK
        WHOLE, HEAD, MIDDLE, BOTH, TAIL = (0, T), (0, T - 2), (T - 2, T - 1), (0, T - 1), (T - 1, T)
        LATE = [(HEAD, c) for c in range(C1 + C2)] + [(MIDDLE, c) for c in range(C1 + C2)] + \
               [(TAIL, c) for c in range(C1)] + [(BOTH, C1 + C2)] + [(TAIL, c) for c in range(C1, LAYERS)]

        def columns(tiles):
            return slice(tiles[0] * P, tiles[1] * P)

        def late_ready(n):
            return 1 + (BLOCKS - 1) * LAYERS + n + 1

        def late_out(who, n):
            return 1 + (BLOCKS - 1) * (DVE_LAYERS, ACT_LAYERS)[who] + sum(c % 2 == who for _, c in LATE[:n + 1])

        def late_bank(n):
            tiles, c = LATE[n]
            if tiles is TAIL and c in (2, 3):
                return turned[c - 2][:, :, :].rearrange("p t s -> p (t s)")
            return chosen_ps[:, :] if tiles is BOTH else layer_ps[c % 2][:, :]

        def chosen_slot(b, k):
            return 2 * k + b % 2 if k < DOUBLED else DOUBLED + k

        def all_blocks(eng, steps):
            steps(0, FIRST)
            with eng.Fori(1, BLOCKS - 1) as b:
                steps(b, BETWEEN)
            steps(BLOCKS - 1, LAST)

        block = ctx.enter_context(nc.Block())

        @block.sync
        def _(sp):
            sp.dma_start(ids_all[:, :, :], ids_v).then_inc(ids_in, 16)
            sp.dma_start(x_rows, x_v).then_inc(x_in, 16)
            for k, t in enumerate(SELECTED):
                if k >= 2:
                    sp.wait_ge(table_hi_ready, k - 1)
                    sp.wait_ge(table_lo_ready, k - 1)
                sp.dma_start(raw[k % 2][0:CP, :], tables[t].rearrange("(p c) d -> p (c d)", p=CP))\
                  .then_inc(raw_in[k % 2], 16)
            sp.dma_start(w1x[:, 0, :], W_top1[0:P, :]).then_inc(w_in, 16)
            sp.dma_start(w1x[:, 1, :], W_top1[P + PAIRS:2 * P + PAIRS, :]).then_inc(w_in, 16)
            sp.dma_start(w1p[0:PC, :, :], W_top1[P:P + PAIRS, :].rearrange("(c p) n -> p c n", p=PC))\
              .then_inc(w_in, 16)
            sp.dma_start(w2[:, :, :], W_top2.rearrange("(c p) n -> p c n", p=P)).then_inc(w_in, 16)
            sp.dma_start(w3[:, :], W_top3.rearrange("(c p) o -> p (c o)", p=P),
                         allow_slow_non_contiguous=True).then_inc(w_in, 16)
            sp.dma_start(b1[:, :], b_top1.rearrange("(c p) -> p c", p=P),
                         allow_slow_non_contiguous=True).then_inc(w_in, 16)
            sp.dma_start(b2[:, :], b_top2.rearrange("(c p) -> p c", p=P),
                         allow_slow_non_contiguous=True).then_inc(w_in, 16)

            def steps(b):
                for t in range(TILES_PER_BLOCK):
                    for c in range(CHUNKS):
                        wait(sp, pairs_in[t][c], b, 16 * LOADS_OF[c], 0)
                        sp.sem_inc(sp_passed, 1)
                    for who in range(2):
                        wait(sp, products_out[who], b, BATCHES_PER_BLOCK // 2, BATCHES // 2 * (t + 1))
                    sp.sem_inc(sp_passed, 1)
                    cells = gram_dram[t].rearrange("(f g) (i q) -> i f g q", g=COLS, i=QUAD)
                    for i in range(QUAD):
                        sp.dma_start(cells[i], gram[FIELDS * i:FIELDS * (i + 1), t % 2, i, :, :])\
                          .then_inc(gram_stored, 16)
                    wait(sp, gram_stored, b, 16 * QUAD * TILES_PER_BLOCK, 16 * QUAD * (t + 1))
                    sp.sem_inc(sp_passed, 1)
                    if t == 1:
                        wait(sp, layer_ready, b, LAYERS, C1 + 1 - LAYERS)
                        sp.sem_inc(sp_passed, 1)
                        bring_back(0)
                    if t >= 1:
                        bring_back(t)

            def bring_back(t):
                cells = gram_dram[t]
                for f0, fields, width, c, row in LOADS:
                    sp.dma_start(pairs[row:row + fields * width, c, t * P:(t + 1) * P],
                                 cells[f0 * FIELDS:f0 * FIELDS + max(width, fields * FIELDS), :]
                                 .rearrange("(f w) s -> f w s", f=fields)[:, 0:width]).then_inc(pairs_in[t][c], 16)

            steps(0)
            with sp.Fori(1, BLOCKS) as b:
                steps(b)
            sp.wait_ge(layer_out[0], late_out(0, len(LATE) - 1))
            sp.dma_start(out_v, y_all[:, :]).then_inc(out_done, 16)
            sp.wait_ge(out_done, 16)

        @block.gpsimd
        def _(pool):
            nc.gpsimd.memset(ident[:, :], 0.0).then_inc(ident_clear, 1)
            pool.wait_ge(ident_clear, 1)
            nc.gpsimd.affine_select(out=ident[:, :], in_=ident[:, :], compare_op=ALU.not_equal, fill=1.0,
                                    base=0, pattern=[[-1, P]], channel_multiplier=1).then_inc(ident_ready, 1)
            nc.gpsimd.iota(row_int[:, :], pattern=[[1, CELLS]], base=0, channel_multiplier=CELLS)\
              .then_inc(row_int_ready, 1)
            pool.wait_ge(ids_in, 16)

            def steps(b):
                for j in range(TILES_PER_BLOCK):
                    if j % 2 == 0:
                        wait(pool, lots_turned, b, LOTS_PER_BLOCK, BLOCKS + NL * (j - 2))
                        nc.gpsimd.tensor_copy(ids_now[:, j:j + 2, :],
                                              ids_all[:, bass.ds(b * TILES_PER_BLOCK + j, 2), :])\
                          .then_inc(ids_copied, 1)
                    for n, lot in enumerate(LOTS):
                        if n == 0:
                            wait(pool, ids_copied, b, TILES_PER_BLOCK // 2, j // 2 + 1)
                        wait(pool, lots_turned, b, LOTS_PER_BLOCK, BLOCKS + NL * (j - 2) + n + 1)
                        pool.sem_inc(pool_passed, 1)
                        for f in lot:
                            nc.gpsimd.indirect_dma_start(
                                out=rows[:, j % 2, row_slot[f], :], out_offset=None, in_=tables[f - 1],
                                in_offset=bass.IndirectOffsetOnAxis(ap=ids_now[:, j, f - 1:f], axis=0),
                            ).then_inc(landed[j % 2][n], 16)

            steps(0)
            with pool.Fori(1, BLOCKS) as b:
                steps(b)

        def copy_lot(eng, copy, who, b, j, n):
            if n == lots_of(j, who)[0]:
                wait(eng, products_ready, b, BATCHES_PER_BLOCK, BATCHES * (j - 1))
            f0, k = LOTS[n][0], len(LOTS[n])
            wait(eng, lots_turned, b, LOTS_PER_BLOCK, BLOCKS + NL * j + n + 1)
            copy(eT[:, j % 2, :, :, f0:f0 + k].rearrange("p q i f -> p i q f"),
                 turned[who][:, 0:k, :].rearrange("p f (i q) -> p i q f", i=QUAD)).then_inc(eT_filled[who], 1)

        def copy_products(eng, copy, who, b, j, batches):
            for m in batches:
                if m % 2 != who:
                    continue
                if m == who:
                    wait(eng, gram_stored, b, 16 * QUAD * TILES_PER_BLOCK, 16 * QUAD * (j - 1))
                wait(eng, products_ready, b, BATCHES_PER_BLOCK, j * BATCHES + m + 1)
                copy(gram[0:QUAD * FIELDS, j % 2, :, :, m * BATCH:(m + 1) * BATCH].rearrange("p i g k -> p k (i g)"),
                     product[who][0:QUAD * FIELDS, 0:BATCH * QUAD * COLS].rearrange("p (k c) -> p k c", k=BATCH))\
                    .then_inc(products_out[who], 1)

        def result_of(c, tiles):
            if c < C1:
                return h1T[:, c, columns(tiles)], b1[:, c:c + 1]
            return h2T[:, c - C1, columns(tiles)], b2[:, c - C1:c - C1 + 1]

        @block.vector
        def _(dve):
            dve.wait_ge(row_int_ready, 1)
            nc.vector.tensor_copy(row_of[:, :], row_int[:, :]).then_inc(row_of_ready, 1)
            dve.wait_ge(ident_ready, 1)
            nc.vector.tensor_copy(ident_half[:, :], ident[:, :]).then_inc(ident_half_ready, 1)
            dve.wait_ge(ids_in, 16)
            for k, t in enumerate(SELECTED):
                nc.vector.tensor_copy(ids_float[:, k, :], ids_all[:, :, t]).then_inc(ids_float_ready, 1)
            nc.vector.memset(ones_half[:, :], 1.0).then_inc(ones_ready, 1)
            dve.wait_ge(row_of_ready, 1)

            def make_onehots(b, k, cells):
                for c in cells:
                    if c == 0:
                        wait(dve, spread_out, b, NS, k + 1)
                    wait(dve, onehots_used, b, CELLS_PER_BLOCK, k * CELLS + c + 1 - RING)
                    nc.vector.tensor_scalar(onehot[:, (k * CELLS + c) % RING, :], spread[:, k % 2, :], row_of[:, c:c + 1], None,
                                            ALU.is_equal).then_inc(onehots_made, 1)

            def select(b, k):
                make_onehots(b, k, range(LEAD, CELLS))
                if k + 1 < NS:
                    make_onehots(b, k + 1, range(LEAD))

            def lower_part(k):
                dve.wait_ge(table_hi_ready, k + 1)
                nc.vector.tensor_tensor(table_lo[0:CP, k, :, :].rearrange("p c d -> p (c d)"), raw[k % 2][0:CP, :],
                                        table_hi[0:CP, k, :, :].rearrange("p c d -> p (c d)").bitcast(F32),
                                        ALU.subtract).then_inc(table_lo_ready, 1)

            def take_in(k):
                make_onehots(0, k, range(LEAD, CELLS))
                if k + 1 < NS:
                    lower_part(k + 1)
                    make_onehots(0, k + 1, range(LEAD))

            def copy_dense(k):
                dve.wait_ge(lots_turned, k + 1)
                nc.vector.tensor_copy(xT[:, k, :], turned[0][:, :, :].rearrange("p t s -> p (t s)"))\
                  .then_inc(xT_filled[0], 1)

            make_onehots(0, 0, range(LEAD))
            copy_dense(0)
            lower_part(0)
            take_in(0)
            copy_dense(2)
            for who in range(2):
                dve.wait_ge(xT_filled[who], BLOCKS // 2)

            def fill_rest(b, j):
                wait(dve, products_ready, b, BATCHES_PER_BLOCK, BATCHES * (j - 1))
                if j == 0:
                    wait(dve, chosen_out, b, NS, NS)
                nc.vector.tensor_copy(
                    eT[:, j % 2, :, :, 0].rearrange("p q i -> p i q"),
                    xT[:, bass.ds(b, 1), j * P:(j + 1) * P].rearrange("p o (i q) -> p (o i) q", i=QUAD))
                for k, f in enumerate(f for run in SELECTED_RUNS for f in run):
                    last = nc.vector.tensor_copy(
                        eT[:, j % 2, :, :, f].rearrange("p q i -> p i q"),
                        chosen[:, bass.ds(chosen_slot(b, k), 1), j * P:(j + 1) * P]
                        .rearrange("p o (i q) -> p (o i) q", i=QUAD))
                last.then_inc(eT_rest, 1)

            def steps(b, work):
                for j in range(TILES_PER_BLOCK):
                    for n in range(NL):
                        if n in lots_of(j, 0):
                            copy_lot(dve, nc.vector.tensor_copy, 0, b, j, n)
                        if n == 1 and j > 0:
                            fill_rest(b, j)
                        for kind, c in work.get((j, n), []):
                            if kind == "t":
                                take_in(c)
                            if kind == "u":
                                select(b, c)
                            if kind == "s":
                                select(b + 1, c)
                            if kind == "r" and c % 2 == 0:
                                result(b - 1, c)
                            if kind == "h" and c % 2 == 0:
                                late_result(c)
                        if work is not FIRST or j > 0:
                            copy_products(dve, nc.vector.tensor_copy, 0, b, j - 1, batches_at(work, j, n))
                        if ("p", 0) in work.get((j, n), []):
                            make_onehots(b + 1, 0, range(LEAD))
                    if j == 0:
                        fill_rest(b, j)
                    if work is FIRST and j == 0:
                        dve.wait_ge(w_in, 16 * WEIGHTS)
                        nc.vector.tensor_tensor(w1d[:, :], w1x[:, 0, :], w1x[:, 1, :], ALU.add)\
                          .then_inc(w1d_ready, 1)

            def take_out(b, c, tiles, bank):
                n = (tiles[1] - tiles[0]) * P
                if c < C1 + C2:
                    dst, bias = result_of(c, tiles)
                    nc.vector.tensor_scalar(dst, bank[:, 0:n], bias, 0.0, ALU.add, ALU.max)\
                      .then_inc(layer_out[0], 1)
                else:
                    nc.vector.tensor_copy(y_all[:, bass.ds(b * TILES_PER_BLOCK + tiles[0], n // P)],
                                          bank[:, 0:n // P]).then_inc(layer_out[0], 1)

            def result(b, c):
                wait(dve, layer_ready, b, LAYERS, c + 2)
                take_out(b, c, WHOLE, layer_ps[0][:, :])

            def late_result(n):
                dve.wait_ge(layer_ready, late_ready(n))
                take_out(BLOCKS - 1, LATE[n][1], LATE[n][0], late_bank(n))

            all_blocks(dve, steps)
            copy_products(dve, nc.vector.tensor_copy, 0, BLOCKS - 1, TILES_PER_BLOCK - 1, range(BATCHES))
            for n in range(C1, len(LATE)):
                if LATE[n][1] % 2 == 0:
                    late_result(n)

        @block.scalar
        def _(act):
            def make_diagonal(b, k):
                wait(act, spread_ready, b, NS, k)
                for t in range(TILES_PER_BLOCK):
                    last = nc.scalar.activation(diagonal[:, t, :], ident_half[:, :], ACT.Copy,
                                                scale=ids_float[:, k, bass.ds(b * TILES_PER_BLOCK + t, 1)])
                last.then_inc(diagonals_made, 1)

            def copy_spread(b, k):
                wait(act, spread_ready, b, NS, k + 1)
                wait(act, onehots_made, b, CELLS_PER_BLOCK, (k - 1) * CELLS)
                nc.scalar.copy(spread[:, k % 2, :], spread_ps[:, :, :].rearrange("p t s -> p (t s)"))\
                  .then_inc(spread_out, 1)

            def copy_chosen(b, k):
                wait(act, onehots_used, b, CELLS_PER_BLOCK, (k + 1) * CELLS)
                if k in (0, DOUBLED):
                    wait(act, eT_rest, b, TILES_PER_BLOCK, -TILES_PER_BLOCK if k < DOUBLED else 0)
                nc.scalar.copy(chosen[:, bass.ds(chosen_slot(b, k), 1), :].rearrange("p o s -> p (o s)"),
                               chosen_ps[:, :]).then_inc(chosen_out, 1)

            def select(b, k):
                if k + 1 < NS:
                    copy_spread(b, k + 1)
                if k + 2 < NS:
                    make_diagonal(b, k + 2)
                copy_chosen(b, k)

            def split(k):
                act.wait_ge(raw_in[k % 2], 16 * (k // 2 + 1))
                nc.scalar.copy(table_hi[0:CP, k, :, :].rearrange("p c d -> p (c d)"), raw[k % 2][0:CP, :])\
                  .then_inc(table_hi_ready, 1)

            def take_in(k):
                if k + 1 < NS:
                    split(k + 1)
                select(0, k)

            def copy_dense(k):
                act.wait_ge(lots_turned, k + 1)
                nc.scalar.copy(xT[:, k, :], turned[1][:, :, :].rearrange("p t s -> p (t s)"))\
                  .then_inc(xT_filled[1], 1)

            act.wait_ge(ident_half_ready, 1)
            act.wait_ge(ids_float_ready, NS)
            make_diagonal(0, 0)
            copy_spread(0, 0)
            make_diagonal(0, 1)
            split(0)
            copy_dense(1)
            take_in(0)
            copy_dense(3)

            def take_out(c, tiles, bank):
                dst, bias = result_of(c, tiles)
                nc.scalar.activation(dst, bank[:, 0:(tiles[1] - tiles[0]) * P], ACT.Relu, bias=bias)\
                  .then_inc(layer_out[1], 1)

            def result(b, c):
                wait(act, layer_ready, b, LAYERS, c + 2)
                take_out(c, WHOLE, layer_ps[1][:, :])

            def late_result(n):
                act.wait_ge(layer_ready, late_ready(n))
                take_out(LATE[n][1], LATE[n][0], late_bank(n))

            def steps(b, work):
                for j in range(TILES_PER_BLOCK):
                    for n in range(NL):
                        if n in lots_of(j, 1):
                            copy_lot(act, nc.scalar.copy, 1, b, j, n)
                        for kind, c in work.get((j, n), []):
                            if kind == "t":
                                take_in(c)
                            if kind == "p":
                                copy_spread(b + 1, 0)
                                make_diagonal(b + 1, 1)
                            if kind == "u":
                                select(b, c)
                            if kind == "s":
                                select(b + 1, c)
                            if kind == "r" and c % 2 == 1:
                                result(b - 1, c)
                            if kind == "h" and c % 2 == 1:
                                late_result(c)
                        if work is not FIRST or j > 0:
                            copy_products(act, nc.scalar.copy, 1, b, j - 1, batches_at(work, j, n))
                        if ("d", 0) in work.get((j, n), []):
                            make_diagonal(b + 1, 0)
                if work is FIRST:
                    act.wait_ge(w_in, 16 * WEIGHTS)

            all_blocks(act, steps)
            copy_products(act, nc.scalar.copy, 1, BLOCKS - 1, TILES_PER_BLOCK - 1, range(BATCHES))
            for n in range(C1, len(LATE)):
                if LATE[n][1] % 2 == 1:
                    late_result(n)

        @block.tensor
        def _(pe):
            for who in range(2):
                pe.sem_inc(layer_out[who], 1)
            pe.sem_inc(layer_ready, 1)
            def transpose_dense(k):
                if k >= 2:
                    pe.wait_ge(xT_filled[k % 2], k // 2)
                for t in range(TILES_PER_BLOCK):
                    T = k * TILES_PER_BLOCK + t
                    last = nc.tensor.transpose(turned[k % 2][:, t, :], x_rows[:, T * P:(T + 1) * P], ident[:, :])
                last.then_inc(lots_turned, 1)

            def spread_ids(b, k):
                wait(pe, spread_out, b, NS, k)
                wait(pe, diagonals_made, b, NS, k + 1)
                nc.tensor.matmul(spread_ps[:, :, :].rearrange("p t s -> p (t s)"), ones_half[:, :],
                                 diagonal[:, :, :].rearrange("p t s -> p (t s)"),
                                 start=True, stop=True).then_inc(spread_ready, 1)

            def select(b, k):
                if k + 1 < NS:
                    spread_ids(b, k + 1)
                wait(pe, chosen_out, b, NS, k)
                for c in range(CELLS):
                    wait(pe, onehots_made, b, CELLS_PER_BLOCK, k * CELLS + c + 1)
                    for part in (table_hi, table_lo):
                        last = nc.tensor.matmul(chosen_ps[:, :], part[0:CP, k, c, :], onehot[0:CP, (k * CELLS + c) % RING, :],
                                                start=(c == 0 and part is table_hi),
                                                stop=(c == CELLS - 1 and part is table_lo))
                    last.then_inc(onehots_used, 1)

            def transpose_lot(b, j, n):
                lot = LOTS[n]
                wait(pe, landed[j % 2][n], b, 32 * len(lot), 16 * len(lot) * (j // 2 + 1))
                who, before = (NL * j + n) % 2, (NL * j + n) // 2
                wait(pe, eT_filled[who], b, LOTS_PER_BLOCK // 2, before)
                for k, f in enumerate(lot):
                    last = nc.tensor.transpose(turned[who][:, k, :], rows[:, j % 2, row_slot[f], :], ident[:, :])
                last.then_inc(lots_turned, 1)

            def multiply(b, j, batches):
                if 0 in batches:
                    for who in range(2):
                        wait(pe, eT_filled[who], b, LOTS_PER_BLOCK // 2,
                             sum(len(lots_of(t, who)) for t in range(j + 1)))
                    wait(pe, eT_rest, b, TILES_PER_BLOCK, j + 1)
                for m in batches:
                    wait(pe, products_out[m % 2], b, BATCHES_PER_BLOCK // 2, j * BATCHES // 2 + m // 2)
                    for k in range(BATCH):
                        q = m * BATCH + k
                        last = nc.tensor.matmul(product[m % 2][0:QUAD * FIELDS, k * QUAD * COLS:(k + 1) * QUAD * COLS],
                                                eT[:, j % 2, q, :, :].rearrange("p i f -> p (i f)"),
                                                eT[:, j % 2, q, :, 1:FIELDS], start=True, stop=True)
                    last.then_inc(products_ready, 1)

            def pairs_back(b, tiles, chunks):
                for t in range(*tiles):
                    for k in chunks:
                        wait(pe, pairs_in[t][k], b, 16 * LOADS_OF[k], 16 * LOADS_OF[k])

            def dense_of(b, tiles):
                return xT[:, bass.ds(b, 1), tiles[0] * P:tiles[1] * P].rearrange("p o s -> p (o s)")

            def pairs_of(k, tiles):
                return pairs[0:PC, k, tiles[0] * P:tiles[1] * P]

            def from_dense(b, c, tiles, bank):
                nc.tensor.matmul(bank, w1d[:, c * P:(c + 1) * P], dense_of(b, tiles), start=True, stop=False)

            def from_chunk(k, c, tiles, bank):
                return nc.tensor.matmul(bank, w1p[0:PC, k, c * P:(c + 1) * P], pairs_of(k, tiles),
                                        start=False, stop=(k == CHUNKS - 1))

            def from_pairs(c, tiles, bank):
                for k in range(CHUNKS):
                    last = from_chunk(k, c, tiles, bank)
                last.then_inc(layer_ready, 1)

            def second_layer(c, tiles, bank):
                for k in range(C1):
                    last = nc.tensor.matmul(bank, w2[:, k, (c - C1) * P:(c - C1 + 1) * P],
                                            h1T[:, k, columns(tiles)], start=(k == 0), stop=(k == C1 - 1))
                last.then_inc(layer_ready, 1)

            def outputs(tiles, bank):
                for t in range(*tiles):
                    for k in range(C2):
                        at = t - tiles[0]
                        last = nc.tensor.matmul(bank[:, at:at + 1], h2T[:, k, t * P:(t + 1) * P],
                                                w3[:, k:k + 1], start=(k == 0), stop=(k == C2 - 1))
                last.then_inc(layer_ready, 1)

            def result(b, c):
                done = {0: DVE_LAYERS, 1: ACT_LAYERS}
                bank = layer_ps[c % 2][:, :]
                if c < C1:
                    wait(pe, layer_out[c % 2], b, done[c % 2], c // 2 + 1)
                    from_dense(b, c, WHOLE, bank)
                    if c == 0:
                        pairs_back(b, WHOLE, range(CHUNKS))
                    from_pairs(c, WHOLE, bank)
                elif c < C1 + C2:
                    for who in range(2):
                        most = C1 // 2 if who != c % 2 else c // 2
                        wait(pe, layer_out[who], b, done[who], most + 1)
                    second_layer(c, WHOLE, bank)
                else:
                    for who in range(2):
                        wait(pe, layer_out[who], b, done[who], (C1 + C2) // 2 + 1)
                    outputs(WHOLE, bank)

            def wait_for_bank(n):
                who = LATE[n][1] % 2
                before = [m for m in range(n) if LATE[m][1] % 2 == who and LATE[m][0] is not BOTH]
                pe.wait_ge(layer_out[who], late_out(who, before[-1] if before else -1))

            def late_start(n):
                tiles, c = LATE[n]
                if c < 2:
                    wait_for_bank(n)
                from_dense(BLOCKS - 1, c, tiles, late_bank(n)[:, 0:P])

            def late_result(n):
                tiles, c = LATE[n]
                bank = late_bank(n)[:, 0:(tiles[1] - tiles[0]) * P]
                if c < C1:
                    wait_for_bank(n)
                    from_dense(BLOCKS - 1, c, tiles, bank)
                    if c == 0:
                        pairs_back(BLOCKS - 1, tiles, range(CHUNKS))
                    from_pairs(c, tiles, bank)
                elif c < C1 + C2:
                    first = LATE.index((tiles, 0))
                    for who in range(2):
                        pe.wait_ge(layer_out[who], late_out(who, first + C1 - 1))
                    wait_for_bank(n)
                    second_layer(c, tiles, bank)
                else:
                    for who in range(2):
                        pe.wait_ge(layer_out[who], late_out(who, LATE.index((MIDDLE if tiles is BOTH else tiles,
                                                                             C1 + C2 - 1))))
                    if tiles is BOTH:
                        pe.wait_ge(chosen_out, BLOCKS * NS)
                    outputs(tiles, bank)

            def take_in(k):
                pe.wait_ge(table_hi_ready, k + 1)
                pe.wait_ge(table_lo_ready, k + 1)
                select(0, k)

            pe.wait_ge(ones_ready, 1)
            spread_ids(0, 0)
            pe.wait_ge(ident_ready, 1)
            pe.wait_ge(x_in, 16)
            transpose_dense(0)
            transpose_dense(1)
            take_in(0)
            transpose_dense(2)
            transpose_dense(3)
            for who in range(2):
                pe.wait_ge(xT_filled[who], BLOCKS // 2)

            def steps(b, work):
                for j in range(TILES_PER_BLOCK):
                    for n in range(NL):
                        transpose_lot(b, j, n)
                        for kind, c in work.get((j, n), []):
                            if kind == "t":
                                take_in(c)
                            if kind == "p":
                                spread_ids(b + 1, 0)
                            if kind == "u":
                                select(b, c)
                            if kind == "s":
                                select(b + 1, c)
                            if kind == "r":
                                result(b - 1, c)
                            if kind == "h":
                                late_result(c)
                        if work is not FIRST or j > 0:
                            multiply(b, j - 1, batches_at(work, j, n))
                if work is FIRST:
                    pe.wait_ge(w_in, 16 * WEIGHTS)
                    pe.wait_ge(w1d_ready, 1)

            all_blocks(pe, steps)
            multiply(BLOCKS - 1, TILES_PER_BLOCK - 1, range(BATCHES))
            middle, tail = LATE.index((MIDDLE, 0)), LATE.index((TAIL, 0))
            for n in range(C1, middle + C1):
                late_result(n)
            late_start(tail + 2)
            late_start(tail + 3)
            for n in range(middle + C1, tail):
                late_result(n)
            late_start(tail)
            late_start(tail + 1)
            for k in range(CHUNKS):
                pairs_back(BLOCKS - 1, TAIL, [k])
                for c in range(C1):
                    last = from_chunk(k, c, TAIL, late_bank(tail + c)[:, 0:P])
                    if k == CHUNKS - 1:
                        last.then_inc(layer_ready, 1)
            for n in range(tail + C1, len(LATE)):
                late_result(n)

    return nc


def kernel(**inputs):
    import concourse.bacc as bacc
    from concourse.bass_utils import run_bass_kernel_spmd

    names = ["r_dense_features", "ids"] + [f"tbl_{t}" for t in range(TABLES)] + \
            ["W_top1", "b_top1", "W_top2", "b_top2", "W_top3"]
    nc = bacc.Bacc("TRN2", target_bir_lowering=False, num_devices=1)
    arrays, aps = {}, {}
    for name in names:
        a = np.ascontiguousarray(inputs[name])
        if name == "W_top1":
            a = a[np.concatenate([np.arange(P), P + np.array(pair_order()), np.arange(P + PAIRS, a.shape[0])])]
        arrays[f"in_{name}"] = a
        aps[name] = nc.dram_tensor(f"in_{name}", a.shape, mybir.dt.from_np(a.dtype), kind="ExternalInput").ap()
    out = nc.dram_tensor("out_y", [inputs["ids"].shape[0], 1], F32, kind="ExternalOutput").ap()
    dlrm_tower(nc, aps["r_dense_features"], aps["ids"], [aps[f"tbl_{t}"] for t in range(TABLES)],
               aps["W_top1"], aps["b_top1"], aps["W_top2"], aps["b_top2"], aps["W_top3"], out)
    return run_bass_kernel_spmd(nc, [arrays], core_ids=[0]).results[0]["out_y"]
```
